# Optimizing a Trainium2 kernel written in Bass

```python
import numpy as np
import jax
import jax.numpy as jnp

def _softmax(x, axis=-1):
    return jax.nn.softmax(x, axis=axis)

def _gelu(x):
    return jax.nn.gelu(x, approximate=True)

def _silu(x):
    return jax.nn.silu(x)

def _sigmoid(x):
    return jax.nn.sigmoid(x)

def _layernorm(x, axis=-1, eps=1e-05):
    m = jnp.mean(x, axis=axis, keepdims=True)
    v = jnp.var(x, axis=axis, keepdims=True)
    return (x - m) / jnp.sqrt(v + eps)

def _scatter_add(tgt, idx, src, axis=0):
    return tgt.at[idx].add(src)

def _segment_sum(src, seg, n):
    return jax.ops.segment_sum(src, seg, n)
kernel_name = 'mk_metaformer_d1_conv_nchw384_r4_bbacc4'

def setup_inputs(seed: int=0):
    np.random.seed(seed)
    _w = jnp.asarray

    def _rec_inputs():
        import jax
        import jax.numpy as jnp
        _gk = jax.random.key(seed)
        x = -0.0001372 + 0.9999 * jax.random.normal(jax.random.fold_in(_gk, 1), (4, 96, 56, 56), jnp.float32)
        return x
    x = _rec_inputs()

    def _L0_conv_setup():
        import jax, jax.numpy as jnp
        import numpy as np
        SP = 8

        def unfold3(x):
            b, c, hc, wc = x.shape
            xp = jnp.pad(x, ((0, 0), (0, 0), (1, 1), (1, 1)))
            return jnp.stack([xp[:, :, i:i + hc, j:j + wc] for i in range(3) for j in range(3)], axis=2)

        def fold3(y):
            b, _, hc, wc = y.shape
            yp = jnp.pad(y, ((0, 0), (0, 0), (1, 1), (1, 1)))
            out = jnp.zeros((b, hc, wc), y.dtype)
            for k2, (i, j) in enumerate([(i, j) for i in range(3) for j in range(3)]):
                out = out + yp[:, k2, 2 - i:2 - i + hc, 2 - j:2 - j + wc]
            return out

        def _stoken_forward(xs, qkv_w, proj_w, proj_b):
            B, C, H, W = xs.shape
            heads = 8
            hd = C // heads
            hh, ww = (H // SP, W // SP)
            n, p = (hh * ww, SP * SP)
            scale = C ** (-0.5)
            xg = xs.reshape(B, C, hh, SP, ww, SP)
            pix = xg.transpose(0, 2, 4, 3, 5, 1).reshape(B, n, p, C)
            sf = xg.mean(axis=(3, 5))
            sf9 = unfold3(sf).reshape(B, C, 9, n).transpose(0, 3, 1, 2)
            aff = jax.nn.softmax(jnp.einsum('bnpc,bnck->bnpk', pix, sf9) * scale, axis=-1)
            aff = jax.lax.stop_gradient(aff)
            aff_sum = fold3(aff.sum(2).transpose(0, 2, 1).reshape(B, 9, hh, ww))[:, None]
            sft = jnp.einsum('bnpc,bnpk->bnck', pix, aff)
            sft = fold3(sft.transpose(0, 2, 3, 1).reshape(B * C, 9, hh, ww)).reshape(B, C, hh, ww)
            sft = sft / (aff_sum + 1e-12)
            qkv = jnp.einsum('oc,bchw->bohw', qkv_w, sft).reshape(B, heads, 3 * hd, n)
            q, k, v = jnp.split(qkv, 3, axis=2)
            attn = jnp.einsum('bhdn,bhdm->bhnm', k, q) * hd ** (-0.5)
            attn = jax.nn.softmax(attn, axis=-2)
            out = jnp.einsum('bhdn,bhnm->bhdm', v, attn).reshape(B, C, hh, ww)
            out = jnp.einsum('oc,bchw->bohw', proj_w, out) + proj_b[None, :, None, None]
            sf9 = unfold3(out).reshape(B, C, 9, n).transpose(0, 3, 1, 2)
            pix_out = jnp.einsum('bnck,bnpk->bncp', sf9, aff)
            return pix_out.reshape(B, hh, ww, C, SP, SP).transpose(0, 3, 1, 4, 2, 5).reshape(B, C, H, W)
        key = jax.random.key(seed)
        ks = jax.random.split(key, 3)
        B, C, H, W = (4, 96, 56, 56)
        xs = jax.random.normal(ks[0], (B, C, H, W), jnp.float32)
        xl = jnp.zeros((1,), jnp.float32)
        qkv_w = jax.random.normal(ks[1], (3 * C, C), jnp.float32) * 0.02
        proj_w = jax.random.normal(ks[2], (C, C), jnp.float32) * 0.02
        proj_b = jnp.zeros((C,), jnp.float32)
        return {'xs': xs, 'xl': xl, 'qkv_w': qkv_w, 'proj_w': proj_w, 'proj_b': proj_b}
    _L0_conv_all = _L0_conv_setup()
    _L0_conv_in = {k: v for k, v in _L0_conv_all.items() if k in ('xl', 'qkv_w', 'proj_w', 'proj_b')}
    del _L0_conv_all

    def _L0_ffn_setup():
        import jax, jax.numpy as jnp
        import numpy as np
        NUM_EXPERTS = 4
        TOP_K = 2
        DIM = 96
        HID = 4 * DIM
        key = jax.random.key(seed)
        ks = jax.random.split(key, 5)
        B, S = (16, 512)
        scale_in = 1.0 / np.sqrt(DIM)
        scale_hid = 1.0 / np.sqrt(HID)
        return {'x': jax.random.normal(ks[0], (B, S, DIM), dtype=jnp.float32), 'gate_w': jax.random.normal(ks[1], (DIM, NUM_EXPERTS), dtype=jnp.float32) * scale_in, 'gate_b': jnp.zeros((NUM_EXPERTS,), dtype=jnp.float32), 'w1': jax.random.normal(ks[2], (NUM_EXPERTS, DIM, HID), dtype=jnp.float32) * scale_in, 'b1': jnp.zeros((NUM_EXPERTS, HID), dtype=jnp.float32), 'w2': jax.random.normal(ks[3], (NUM_EXPERTS, HID, DIM), dtype=jnp.float32) * scale_hid, 'b2': jnp.zeros((NUM_EXPERTS, DIM), dtype=jnp.float32)}
    _L0_ffn_all = _L0_ffn_setup()
    _L0_ffn_in = {k: v for k, v in _L0_ffn_all.items() if k in ('gate_w', 'gate_b', 'w1', 'b1', 'w2', 'b2')}
    del _L0_ffn_all
    return {'x': x, 'L0_conv_xl': _L0_conv_in['xl'], 'L0_conv_qkv_w': _L0_conv_in['qkv_w'], 'L0_conv_proj_w': _L0_conv_in['proj_w'], 'L0_conv_proj_b': _L0_conv_in['proj_b'], 'L0_ffn_gate_w': _L0_ffn_in['gate_w'], 'L0_ffn_gate_b': _L0_ffn_in['gate_b'], 'L0_ffn_w1': _L0_ffn_in['w1'], 'L0_ffn_b1': _L0_ffn_in['b1'], 'L0_ffn_w2': _L0_ffn_in['w2'], 'L0_ffn_b2': _L0_ffn_in['b2']}

def reference(x, L0_conv_xl, L0_conv_qkv_w, L0_conv_proj_w, L0_conv_proj_b, L0_ffn_gate_w, L0_ffn_gate_b, L0_ffn_w1, L0_ffn_b1, L0_ffn_w2, L0_ffn_b2):
    import jax
    import jax.numpy as jnp

    def _L0_conv_ref(xs, xl, qkv_w, proj_w, proj_b):
        import jax, jax.numpy as jnp
        import numpy as np
        SP = 8

        def unfold3(x):
            b, c, hc, wc = x.shape
            xp = jnp.pad(x, ((0, 0), (0, 0), (1, 1), (1, 1)))
            return jnp.stack([xp[:, :, i:i + hc, j:j + wc] for i in range(3) for j in range(3)], axis=2)

        def fold3(y):
            b, _, hc, wc = y.shape
            yp = jnp.pad(y, ((0, 0), (0, 0), (1, 1), (1, 1)))
            out = jnp.zeros((b, hc, wc), y.dtype)
            for k2, (i, j) in enumerate([(i, j) for i in range(3) for j in range(3)]):
                out = out + yp[:, k2, 2 - i:2 - i + hc, 2 - j:2 - j + wc]
            return out

        def _stoken_forward(xs, qkv_w, proj_w, proj_b):
            B, C, H, W = xs.shape
            heads = 8
            hd = C // heads
            hh, ww = (H // SP, W // SP)
            n, p = (hh * ww, SP * SP)
            scale = C ** (-0.5)
            xg = xs.reshape(B, C, hh, SP, ww, SP)
            pix = xg.transpose(0, 2, 4, 3, 5, 1).reshape(B, n, p, C)
            sf = xg.mean(axis=(3, 5))
            sf9 = unfold3(sf).reshape(B, C, 9, n).transpose(0, 3, 1, 2)
            aff = jax.nn.softmax(jnp.einsum('bnpc,bnck->bnpk', pix, sf9) * scale, axis=-1)
            aff = jax.lax.stop_gradient(aff)
            aff_sum = fold3(aff.sum(2).transpose(0, 2, 1).reshape(B, 9, hh, ww))[:, None]
            sft = jnp.einsum('bnpc,bnpk->bnck', pix, aff)
            sft = fold3(sft.transpose(0, 2, 3, 1).reshape(B * C, 9, hh, ww)).reshape(B, C, hh, ww)
            sft = sft / (aff_sum + 1e-12)
            qkv = jnp.einsum('oc,bchw->bohw', qkv_w, sft).reshape(B, heads, 3 * hd, n)
            q, k, v = jnp.split(qkv, 3, axis=2)
            attn = jnp.einsum('bhdn,bhdm->bhnm', k, q) * hd ** (-0.5)
            attn = jax.nn.softmax(attn, axis=-2)
            out = jnp.einsum('bhdn,bhnm->bhdm', v, attn).reshape(B, C, hh, ww)
            out = jnp.einsum('oc,bchw->bohw', proj_w, out) + proj_b[None, :, None, None]
            sf9 = unfold3(out).reshape(B, C, 9, n).transpose(0, 3, 1, 2)
            pix_out = jnp.einsum('bnck,bnpk->bncp', sf9, aff)
            return pix_out.reshape(B, hh, ww, C, SP, SP).transpose(0, 3, 1, 4, 2, 5).reshape(B, C, H, W)
        return _stoken_forward(xs, qkv_w, proj_w, proj_b)

    def _L0_ffn_ref(x, gate_w, gate_b, w1, b1, w2, b2):
        import jax, jax.numpy as jnp
        import numpy as np
        NUM_EXPERTS = 4
        TOP_K = 2
        DIM = 96
        HID = 4 * DIM
        scores = jnp.einsum('bsd,de->bse', x, gate_w) + gate_b
        probs = jax.nn.softmax(scores, axis=-1)
        topk_vals, topk_idx = jax.lax.top_k(probs, TOP_K)
        mask = jnp.sum(jax.nn.one_hot(topk_idx, NUM_EXPERTS, dtype=probs.dtype), axis=-2)
        masked = probs * mask
        masked = masked / (jnp.sum(masked, axis=-1, keepdims=True) + 1e-09)
        h = jax.nn.gelu(jnp.einsum('bsd,edh->ebsh', x, w1) + b1[:, None, None, :], approximate=False)
        y = jnp.einsum('ebsh,ehd->ebsd', h, w2) + b2[:, None, None, :]
        out = jnp.einsum('bse,ebsd->bsd', masked, y)
        return out

    def _gn(v, G=32, eps=1e-05):
        B_, C_, H_, W_ = v.shape
        g = v.reshape(B_, G, C_ // G, H_, W_)
        m = jnp.mean(g, axis=(2, 3, 4), keepdims=True)
        s = jnp.var(g, axis=(2, 3, 4), keepdims=True)
        return ((g - m) / jnp.sqrt(s + eps)).reshape(v.shape)

    def _ln_c(v, eps=1e-06):
        m = jnp.mean(v, axis=1, keepdims=True)
        s = jnp.var(v, axis=1, keepdims=True)
        return (v - m) / jnp.sqrt(s + eps)

    def _ln_t(v, eps=1e-05):
        m = jnp.mean(v, axis=-1, keepdims=True)
        s = jnp.var(v, axis=-1, keepdims=True)
        return (v - m) / jnp.sqrt(s + eps)

    def _to_tokens(v):
        B_, C_, H_, W_ = v.shape
        return v.reshape(B_, C_, H_ * W_).transpose(0, 2, 1)

    def _from_tokens(t, like):
        B_, C_, H_, W_ = like.shape
        return t.transpose(0, 2, 1).reshape(B_, C_, H_, W_)
    x = x + _L0_conv_ref(_ln_c(x), L0_conv_xl, L0_conv_qkv_w, L0_conv_proj_w, L0_conv_proj_b)
    t = _to_tokens(x)
    t = t + _L0_ffn_ref(_ln_t(t), L0_ffn_gate_w, L0_ffn_gate_b, L0_ffn_w1, L0_ffn_b1, L0_ffn_w2, L0_ffn_b2)
    x = _from_tokens(t, x)
    return x

_drawn_inputs = setup_inputs


def setup_inputs(seed=0):
    import zlib

    import numpy as np

    out = dict(_drawn_inputs(seed))
    spreads = {'L0_conv_proj_b': (0.0, 0.1),
     'L0_ffn_gate_b': (0.0, 0.1),
     'L0_ffn_b1': (0.0, 0.1),
     'L0_ffn_b2': (0.0, 0.1)}
    factors = {'L0_conv_qkv_w': 8.0, 'L0_conv_proj_w': 8.0}
    for name, (base, spread) in spreads.items():
        noise = np.random.default_rng([zlib.crc32(name.encode()), seed]).standard_normal(out[name].shape)
        drawn = base * np.exp(spread * noise) if base else spread * noise
        out[name] = jnp.asarray(drawn.astype(out[name].dtype))
    for name, factor in factors.items():
        out[name] = (out[name] * factor).astype(out[name].dtype)
    return out
```

```python
from contextlib import ExitStack

import numpy as np

import concourse.bass as bass
from concourse import mybir

F32 = mybir.dt.float32
F16 = mybir.dt.float16
ALU = mybir.AluOpType
ACT = mybir.ActivationFunctionType
AX = mybir.AxisListType

B, C, H, W = 4, 96, 56, 56
SP = 8
G = H // SP
GP = G + 2
N = G * G
K9 = 3 * GP
PT = 2 * W
TU = SP * W // PT
UT = TU * PT
U = B * G
T = G * TU
IMG = H * W
TOK = B * IMG
HEADS = 8
HD = C // HEADS
E = 4
HID = 4 * C
CH = HID // 128
CB = C + 1
WS = 64.0
BANK = 512
ZONE = 32
NEG = -1.0e30


def constants():
    p = np.arange(128)
    cell = (p % W) // SP + 1
    col = np.arange(GP)
    near = np.where(np.abs(col[None] - cell[:, None]) <= 1, 0.0, NEG)
    mean = (col[None] == cell[:, None]) / float(SP * SP)
    e = np.arange(E)
    below = np.tile((e[None, :] < e[:, None]).reshape(1, E * E), (128, 1))
    rank = np.tile((e - 1.5)[None], (128, 1))
    table = np.concatenate([np.eye(128), np.tile(near, (1, 3)), mean, below, rank], axis=1)
    inner = np.zeros((GP, GP))
    inner[1:-1, 1:-1] = 1.0
    row = np.tile(np.concatenate([inner.reshape(-1), np.zeros(9)]), (1, B))
    return table.astype(np.float32), row.astype(np.float32)


AW = GP * GP + 9


def build(nc, x, table, inner, wqkv, wproj, bproj, gate_w, gate_b, w1, b1, w2, b2, mid, gates, out):
    with ExitStack() as ctx:
        def sb(name, shape, dt=F32):
            return ctx.enter_context(nc.sbuf_tensor(name, shape, dt))

        def sem(name):
            return ctx.enter_context(nc.semaphore(name))

        tab = sb("tab", [128, table.shape[1]])
        o = 0
        ident = tab[:, 0:128]
        o = 128
        near = tab[:, o:o + K9]
        o += K9
        cellmean = tab[:, o:o + GP]
        o += GP
        below = tab[:, o:o + E * E]
        o += E * E
        rankmax = tab[:, o:o + E]
        ident16 = sb("ident16", [128, 128], F16)
        wqkv_sb = sb("wqkv_sb", [C, 3 * C])
        wproj_sb = sb("wproj_sb", [CB, C])
        gate_hi = sb("gate_hi", [CB, E], F16)
        gate_lo = sb("gate_lo", [CB, E], F16)
        w1_hi = sb("w1_hi", [CB, E * HID], F16)
        w1_lo = sb("w1_lo", [CB, E * HID], F16)
        w2_hi = sb("w2_hi", [128, E * CH, C], F16)
        w2_lo = sb("w2_lo", [128, E * CH, C], F16)
        b2_sb = sb("b2_sb", [C, E])
        gate_st = sb("gate_st", [CB, E])

        xc = sb("xc", [C, 2, IMG])
        xt = sb("xt", [PT, 2, T, CB])
        st = sb("st", [PT, T, 6])
        mom = sb("mom", [PT, 5, T])
        rstd = sb("rstd", [PT, T])
        minus_half = sb("minus_half", [PT, 1])
        sf = sb("sf", [C, GP * GP])
        aff = sb("aff", [PT, T, K9])
        affs = sb("affs", [PT, 2, T])
        aff16 = sb("aff16", [PT, T, 3 * ZONE], F16)
        affT = sb("affT", [3 * ZONE, TOK], F16)
        sft = sb("sft", [CB, B * N])
        zeros = sb("zeros", [PT, CB])
        sftT = sb("sftT", [N, B, C])
        srec = sb("srec", [N, B])
        sfn = sb("sfn", [C, B, N])
        q = sb("q", [HD, HEADS, B * N])
        k = sb("k", [HD, HEADS, B * N])
        vT = sb("vT", [N, B, C])
        xh = sb("xh", [CB, TOK], F16)
        xl = sb("xl", [CB, TOK], F16)
        ao = sb("ao", [N, B, C])
        aoT = sb("aoT", [CB, B, AW])
        so = sb("so", [3 * ZONE, U, C], F16)
        asm = sb("asm", [N, 3, B * HEADS])
        gl = sb("gl", [PT, T, E])
        gs = sb("gs", [PT, 4, T])
        gc = sb("gc", [PT, T, E * E])
        ga = sb("ga", [PT, 2, T, E])
        gT = sb("gT", [T * E, PT])
        big = sb("big", [128, 8 * CH * UT], F16)
        w1_st = big[0:CB, 0:2 * E * HID].bitcast(F32)
        w2_st = big[:, 2 * E * HID:2 * E * HID + 2 * E * CH * C].bitcast(F32)
        prob = big[0:N, 0:2 * B * HEADS * N].bitcast(F32).rearrange("p (b h n) -> p b h n", b=B, h=HEADS)
        probT = big[0:N, 2 * B * HEADS * N:4 * B * HEADS * N].bitcast(F32).rearrange(
            "p (b h n) -> p b h n", b=B, h=HEADS)
        HW_ = CH * UT
        h32 = [big[:, 2 * i * HW_:2 * (i + 1) * HW_].bitcast(F32).rearrange("p (c n) -> p c n", c=CH)
               for i in range(2)]
        hh = [big[:, (4 + i) * HW_:(5 + i) * HW_].rearrange("p (c n) -> p c n", c=CH) for i in range(2)]
        hl = [big[:, (6 + i) * HW_:(7 + i) * HW_].rearrange("p (c n) -> p c n", c=CH) for i in range(2)]
        spare = xc[:, :, :].rearrange("p a n -> p (a n)")
        assert E * UT * 2 + UT * 6 <= 2 * IMG
        gb = [spare[:, i * E * UT:(i + 1) * E * UT].rearrange("p (e n) -> p e n", e=E) for i in range(2)]
        o = 2 * E * UT
        tb = [spare[:, o + i * UT:o + (i + 1) * UT] for i in range(2)]
        res = [spare[:, o + (2 + i) * UT:o + (3 + i) * UT] for i in range(2)]
        acc = [spare[:, o + (4 + i) * UT:o + (5 + i) * UT] for i in range(2)]

        ps = ctx.enter_context(nc.psum_tensor("ps", [128, 8, BANK], F32))

        names = """consts_in x_in0 x_in1 init_done pool_init weights_ready split_step
            xT_done xT_copied moments_ready rstd_ready xn_ready sf_done sf_ready xnC_done xnC_ready
            logits_done shifted exp_ready aff_ready aff_hi aff_lo sft_done sft_ready affT_done affT_ready
            attn_pe attn_dve attn_act attn_step norm1_step norm3_step
            pix_done mid_ready mid_stored tT_done tT_copied x2_ready x2C_done xh_ready xl_ready
            gate_done gate_shifted gate_exp gate_ready gT_done gT_copied gates_out
            z_done hh_ready h_ready hl_ready y_done y_free unit_in0 unit_in1 part_ready sum_ready res_ready
            out_stored0 out_stored1""".split()
        S = {n: sem(n) for n in names}
        N_CONST = 11

        block = ctx.enter_context(nc.Block())

        def images(eng):
            with eng.Fori(0, B // 2) as pair:
                for par in range(2):
                    yield pair * 2 + par, par

        def unit_cols(u):
            return bass.ds(u * UT, UT)

        def rowcols(b, r):
            return bass.ds(b * IMG + r * UT, UT)

        def store_mid(sp, b):
            sp.wait_ge(S["mid_ready"], G * (b + 1))
            sp.dma_start(mid[:, b * IMG:(b + 1) * IMG], xc[:, b % 2, :]).then_inc(S["mid_stored"], 16)

        @block.sync
        def _(sp):
            def load_image(b):
                sp.dma_start(xc[:, b % 2, :], x[:, b * IMG:(b + 1) * IMG]).then_inc(S[f"x_in{b % 2}"], 16)

            load_image(0)
            for dst, src in ((tab[:], table), (wqkv_sb[:], wqkv), (wproj_sb[0:C, :], wproj),
                             (wproj_sb[C:CB, :], bproj), (gate_st[0:C, :], gate_w), (gate_st[C:CB, :], gate_b),
                             (w1_st[0:C, :], w1), (w1_st[C:CB, :], b1), (w2_st, w2), (b2_sb[:], b2)):
                sp.dma_start(dst, src).then_inc(S["consts_in"], 16)
            load_image(1)
            sp.wait_ge(S["init_done"], 1)
            sp.dma_start(aoT[C:CB, :, :], inner.rearrange("o (b n) -> o b n", b=B)).then_inc(S["consts_in"], 16)
            for b in range(2, B):
                sp.wait_ge(S["logits_done"], b - 1)
                load_image(b)
            for b in range(B):
                if b < 2:
                    sp.wait_ge(S["logits_done"], b + 3)
                else:
                    sp.wait_ge(S["tT_done"], G * (b - 1))
                    sp.wait_ge(S["mid_stored"], 16 * (b - 1))
                load_image(b)
                if b >= 1:
                    store_mid(sp, b - 1)
            store_mid(sp, B - 1)
            sp.wait_ge(S["mid_stored"], 16 * B)
            sp.wait_ge(S["gates_out"], 16 * B)
            sp.wait_ge(S["tT_done"], G * B)

            def load_unit(u, par):
                sp.dma_start(tb[par], mid[:, unit_cols(u)]).then_inc(S[f"unit_in{par}"], 16)
                sp.dma_start(gb[par], gates[:, unit_cols(u)].unsqueeze(0).to_broadcast([C, E, UT])
                             ).then_inc(S[f"unit_in{par}"], 16)

            def store_unit(u, par):
                sp.wait_ge(S["res_ready"], u + 1)
                sp.dma_start(out[:, unit_cols(u)], res[par]).then_inc(S[f"out_stored{par}"], 16)

            load_unit(0, 0)
            load_unit(1, 1)
            with sp.Fori(0, U // 2 - 1) as pair:
                for par in range(2):
                    store_unit(pair * 2 + par, par)
                    load_unit(pair * 2 + par + 2, par)
            for par in range(2):
                store_unit(U - 2 + par, par)
            for par in range(2):
                sp.wait_ge(S[f"out_stored{par}"], 16 * (U // 2) + 1)

        @block.gpsimd
        def _(pool):
            for n, (what, value) in enumerate(((xt[:, :, :, C:CB], 1.0), (minus_half[:], -0.5),
                                               (xh[C:CB, :], 1.0), (xl[C:CB, :], 0.0))):
                pool.memset(what, value).then_inc(S["pool_init"], 1)
                pool.wait_ge(S["pool_init"], n + 1)
            with pool.Fori(0, 2 * B) as n:
                pool.wait_ge(S["moments_ready"], n + 1)
                pool.tensor_tensor(rstd[:], mom[:, 4, :], minus_half[:].to_broadcast([PT, T]),
                                   ALU.pow).then_inc(S["rstd_ready"], 1)

        @block.scalar
        def _(act):
            act.wait_ge(S["init_done"], 1)
            for b, par in images(act):
                for r in range(G):
                    act.wait_ge(S["xT_done"], b * G + (r + 1))
                    act.copy(xt[:, par, r * TU:(r + 1) * TU, 0:C],
                             ps[0:PT, (G * par + r) % 2, 0:TU * C].rearrange("p (t c) -> p t c", t=TU)
                             ).then_inc(S["xT_copied"], 1)
                for r in range(G):
                    act.wait_ge(S["xnC_done"], b * G + (r + 1))
                    act.copy(xc[:, par, r * UT:(r + 1) * UT], ps[0:C, 3 + (G * par + r) % 2, 0:UT]
                             ).then_inc(S["xnC_ready"], 1)
                act.wait_ge(S["shifted"], b + 1)
                act.activation(aff[:], aff[:], ACT.Exp, scale=float(C) ** -0.5).then_inc(S["exp_ready"], 1)
                act.wait_ge(S["aff_ready"], b + 1)
                for zone in (0, 2):
                    act.copy(aff16[:, :, zone * ZONE:zone * ZONE + K9], aff[:]).then_inc(S["aff_hi"], 1)
                for r in range(G):
                    act.wait_ge(S["affT_done"], b * G + (r + 1))
                    act.copy(affT[:, rowcols(b, r)],
                             ps[0:3 * ZONE, (G * par + r) % 2, 0:UT // 2].bitcast(F16)
                             ).then_inc(S["affT_ready"], 1)
            act.wait_ge(S["attn_pe"], 3)
            act.copy(k[:].rearrange("p (a h) n -> p a (h n)", h=2), ps[0:HD, 4:8, 0:2 * B * N]
                     ).then_inc(S["attn_act"], 1)
            act.wait_ge(S["attn_dve"], 5)
            act.activation(prob, prob, ACT.Exp, scale=float(HD) ** -0.5).then_inc(S["attn_act"], 1)
            for b, par in images(act):
                for r in range(G):
                    act.wait_ge(S["tT_done"], b * G + (r + 1))
                    act.copy(xt[:, par, r * TU:(r + 1) * TU, 0:C],
                             ps[0:PT, 2 + (G * par + r) % 2, 0:TU * C].rearrange("p (t c) -> p t c", t=TU)
                             ).then_inc(S["tT_copied"], 1)
                for r in range(G):
                    act.wait_ge(S["x2C_done"], b * G + (r + 1))
                    act.copy(xh[0:C, rowcols(b, r)], ps[0:C, 4 + (G * par + r) % 2, 0:UT]
                             ).then_inc(S["xh_ready"], 1)
                act.wait_ge(S["gate_shifted"], b + 1)
                act.activation(gl[:], gl[:], ACT.Exp, scale=1.0 / WS).then_inc(S["gate_exp"], 1)
                act.wait_ge(S["gT_done"], b + 1)
                act.copy(gT[:], ps[0:T * E, 7, 0:PT]).then_inc(S["gT_copied"], 1)
                act.wait_ge(S["gT_copied"], b + 1)
                act.dma_start(gates[:, bass.ds(b * IMG, IMG)].rearrange("e (t p) -> t e p", p=PT),
                              gT[:]).then_inc(S["gates_out"], 16)
                act.wait_ge(S["gates_out"], b * 16 + 16)
            with act.Fori(0, U, 4) as u4:
                for ue in range(4 * E):
                    u, e = u4 + ue // E, ue % E
                    z = ps[:, CH * (e % 2):CH * (e % 2) + CH, 0:UT]
                    act.wait_ge(S["z_done"], u * E + (e + 1))
                    act.wait_ge(S["y_done"], u * E + e + 1)
                    act.activation(hh[e % 2], z, ACT.Gelu, scale=1.0 / WS).then_inc(S["hh_ready"], 1)
                    act.activation(h32[e % 2], z, ACT.Gelu, scale=1.0 / WS).then_inc(S["h_ready"], 1)

        @block.vector
        def _(dve):
            class Steps:

                def __init__(self, name):
                    self.sem, self.base, self.n = S[name], 0, 0

                def image(self, b, per):
                    assert self.n in (0, per), self.n
                    self.base, self.n = b * per, 0

                def mark(self, ins):
                    ins.then_inc(self.sem, 1)
                    self.n += 1

                def settle(self):
                    dve.wait_ge(self.sem, self.base + self.n)

                def link(self, ins):
                    self.mark(ins)
                    self.settle()

            s = Steps("split_step")
            s.mark(dve.memset(sf[:], 0.0))
            s.mark(dve.memset(zeros[:], 0.0))
            s.mark(dve.memset(aff16[:], 0.0))
            s.mark(dve.memset(so[:], 0.0))
            for n, (name, start) in enumerate((("y_done", 2), ("y_free", 2), ("h_ready", 1), ("out_stored0", 1),
                                               ("out_stored1", 1))):
                dve.memset(asm[:, 0, n:n + 1], 0.0).then_inc(S[name], start)
            s.settle()
            dve.memset(aoT[:], 0.0).then_inc(S["init_done"], 1)
            dve.wait_ge(S["consts_in"], 16 * N_CONST)
            s.mark(dve.tensor_copy(ident16[:], ident))
            for hi, lo, src in ((gate_hi[:], gate_lo[:], gate_st[:]), (w1_hi[:], w1_lo[:], w1_st),
                                (w2_hi[:].rearrange("p a c -> p (a c)"), w2_lo[:].rearrange("p a c -> p (a c)"),
                                 w2_st)):
                s.link(dve.tensor_scalar(hi, src, WS, None, ALU.mult))
                s.mark(dve.scalar_tensor_tensor(out=lo, in0=src, scalar=WS, in1=hi, op0=ALU.mult,
                                                op1=ALU.subtract))
            s.settle()
            dve.tensor_scalar(b2_sb[:], b2_sb[:], WS, None, ALU.mult).then_inc(S["weights_ready"], 1)
            dve.wait_ge(S["weights_ready"], 1)
            dve.wait_ge(S["pool_init"], 4)

            def moments(s, eps):
                me, mo, qe, qo = (st[:, :, i] for i in (1, 4, 2, 5))
                s.mark(dve.tensor_tensor(mom[:, 1, :], me, mo, ALU.subtract))
                s.mark(dve.tensor_tensor(mom[:, 0, :], me, mo, ALU.add))
                s.link(dve.tensor_tensor(mom[:, 2, :], qe, qo, ALU.add))
                s.mark(dve.scalar_tensor_tensor(out=mom[:, 3, :], in0=mom[:, 1, :], scalar=0.25,
                                                in1=mom[:, 1, :], op0=ALU.mult, op1=ALU.mult))
                s.mark(dve.tensor_scalar(mom[:, 0, :], mom[:, 0, :], 0.5, None, ALU.mult))
                s.link(dve.tensor_scalar(mom[:, 2, :], mom[:, 2, :], 1.0 / C, eps, ALU.mult, ALU.add))
                dve.tensor_tensor(mom[:, 4, :], mom[:, 3, :], mom[:, 2, :], ALU.add).then_inc(
                    S["moments_ready"], 1)

            def statistics(s, b, par, copied):
                for r in range(G):
                    dve.wait_ge(copied, b * G + (r + 1))
                    for j in range(TU):
                        ins = dve.bn_stats(st[:, r * TU + j, :], xt[:, par, r * TU + j, 0:C])
                s.link(ins)

            def normalise(par, ready):
                for r in range(G):
                    for t in range(r * TU, (r + 1) * TU):
                        ins = dve.tensor_scalar(xt[:, par, t, 0:C], xt[:, par, t, 0:C], mom[:, 0, t:t + 1],
                                                rstd[:, t:t + 1], ALU.subtract, ALU.mult)
                    ins.then_inc(ready, 1)

            s = Steps("norm1_step")
            for b, par in images(dve):
                s.image(b, 12)
                statistics(s, b, par, S["xT_copied"])
                moments(s, 1e-6)
                dve.wait_ge(S["rstd_ready"], b + 1)
                normalise(par, S["xn_ready"])
                dve.wait_ge(S["sf_done"], b + 1)
                dve.tensor_copy(sf[:, GP:GP * (G + 1)], ps[0:C, 2, 0:G * GP]).then_inc(S["sf_ready"], 1)
                dve.wait_ge(S["logits_done"], b + 1)
                cut = 4 * TU
                for bank, t0, t1 in ((5, 0, cut), (6, cut, T)):
                    s.mark(dve.tensor_tensor(
                        aff[:, t0:t1, :],
                        ps[0:PT, bank, 0:(t1 - t0) * K9].rearrange("p (t n) -> p t n", n=K9),
                        near[0:PT, :].unsqueeze(1).to_broadcast([PT, t1 - t0, K9]), ALU.add))
                s.settle()
                s.link(dve.tensor_reduce(affs[:, 0, :], aff[:], AX.X, ALU.max))
                dve.tensor_tensor(aff[:], aff[:], affs[:, 0, :].unsqueeze(2).to_broadcast([PT, T, K9]),
                                  ALU.subtract).then_inc(S["shifted"], 1)
                dve.wait_ge(S["exp_ready"], b + 1)
                s.link(dve.tensor_reduce(affs[:, 1, :], aff[:], AX.X, ALU.add))
                s.link(dve.reciprocal(affs[:, 1, :], affs[:, 1, :]))
                dve.tensor_tensor(aff[:], aff[:], affs[:, 1, :].unsqueeze(2).to_broadcast([PT, T, K9]),
                                  ALU.mult).then_inc(S["aff_ready"], 1)
                dve.wait_ge(S["aff_hi"], b * 2 + 1)
                dve.tensor_tensor(aff16[:, :, ZONE:ZONE + K9], aff[:], aff16[:, :, 0:K9],
                                  ALU.subtract).then_inc(S["aff_lo"], 1)
                dve.wait_ge(S["sft_done"], b + 1)
                dve.tensor_copy(sft[:, bass.ds(b * N, N)].rearrange("p (i j) -> p i j", j=G),
                                ps[0:CB, 7, 0:GP * GP].rearrange("p (i j) -> p i j", j=GP)[:, 1:G + 1, 1:G + 1]
                                ).then_inc(S["sft_ready"], 1)
            s.image(0, 12)

            s = Steps("attn_step")

            def grid(bank, rows, cols, n):
                return ps[0:rows, bank, 0:n * cols].rearrange("p (b c) -> p b c", b=n)

            dve.wait_ge(S["attn_pe"], 1)
            sT = grid(0, N, CB, B)
            s.link(dve.tensor_scalar(srec[:], sT[:, :, C], 1e-12, None, ALU.add))
            s.link(dve.reciprocal(srec[:], srec[:]))
            dve.tensor_tensor(sftT[:], sT[:, :, 0:C], srec[:].unsqueeze(2).to_broadcast([N, B, C]),
                              ALU.mult).then_inc(S["attn_dve"], 1)
            dve.wait_ge(S["attn_pe"], 2)
            dve.tensor_copy(sfn[:], grid(1, C, N, B)).then_inc(S["attn_dve"], 1)
            dve.wait_ge(S["attn_pe"], 3)
            dve.tensor_copy(q[:].rearrange("p (a h) n -> p a (h n)", h=2), ps[0:HD, 0:4, 0:2 * B * N]
                            ).then_inc(S["attn_dve"], 1)
            dve.wait_ge(S["attn_pe"], 4)
            dve.tensor_copy(vT[:], grid(0, N, C, B)).then_inc(S["attn_dve"], 1)
            dve.wait_ge(S["attn_pe"], 5)
            sc = ps[0:N, 4:8, 0:HEADS * N].rearrange("p b (h n) -> p b h n", h=HEADS)

            def stat(i):
                return asm[:, i, :].rearrange("p (b h) -> p b h", b=B)

            s.link(dve.tensor_reduce(stat(0), sc, AX.X, ALU.max))
            dve.tensor_tensor(prob, sc, stat(0).unsqueeze(3).to_broadcast([N, B, HEADS, N]),
                              ALU.subtract).then_inc(S["attn_dve"], 1)
            dve.wait_ge(S["attn_act"], 2)
            s.link(dve.tensor_reduce(stat(1), prob, AX.X, ALU.add))
            s.link(dve.reciprocal(asm[:, 2, :], asm[:, 1, :]))
            dve.wait_ge(S["attn_pe"], 6)
            dve.tensor_copy(probT.rearrange("p b h n -> p b (h n)"), ps[0:N, 0:4, 0:HEADS * N]
                            ).then_inc(S["attn_dve"], 1)
            dve.wait_ge(S["attn_pe"], 7)
            dve.tensor_tensor(ao[:].rearrange("p b (h d) -> p (b h) d", h=HEADS),
                              ps[0:N, 4, 0:B * C].rearrange("p (g d) -> p g d", d=HD),
                              asm[:, 2, :].unsqueeze(2).to_broadcast([N, B * HEADS, HD]),
                              ALU.mult).then_inc(S["attn_dve"], 1)
            dve.wait_ge(S["attn_pe"], 8)
            for b in range(B):
                ins = dve.tensor_copy(
                    aoT[0:C, b, 0:GP * GP].rearrange("p (i j) -> p i j", j=GP)[:, 1:G + 1, 1:G + 1],
                    ps[0:C, 5, b * N:(b + 1) * N].rearrange("p (i j) -> p i j", j=G))
            ins.then_inc(S["attn_dve"], 1)
            dve.wait_ge(S["attn_pe"], 9)
            full = BANK // C
            parts = [(0, U // full, 0, U // full * full, full), (U // full, U // full + 1, U // full * full, U, U % full)]
            for hi in (True, False):
                lo_, hi_ = (0, 3 * ZONE) if hi else (2 * ZONE, 3 * ZONE)
                for k0, k1, u0, u1, n in parts:
                    dst = so[lo_:hi_, u0:u1, :].rearrange("p (k n) c -> p k (n c)", n=n)
                    src = ps[lo_:hi_, k0:k1, 0:n * C]
                    if hi:
                        s.mark(dve.tensor_copy(dst, src))
                    else:
                        ins = dve.tensor_tensor(dst, src, dst, ALU.subtract)
                s.settle()
            ins.then_inc(S["attn_dve"], 1)

            s = Steps("norm3_step")
            for b, par in images(dve):
                s.image(b, 21)
                dve.wait_ge(S[f"x_in{par}"], b * 8 + (48 - 8 * par))
                for r in range(G):
                    dve.wait_ge(S["pix_done"], b * G + (r + 1))
                    cols = xc[:, par, r * UT:(r + 1) * UT]
                    dve.tensor_tensor(cols, cols, ps[0:C, (G * par + r) % 2, 0:UT], ALU.add
                                      ).then_inc(S["mid_ready"], 1)
                statistics(s, b, par, S["tT_copied"])
                moments(s, 1e-5)
                dve.wait_ge(S["rstd_ready"], b + (B + 1))
                normalise(par, S["x2_ready"])
                for r in range(G):
                    dve.wait_ge(S["xh_ready"], b * G + (r + 1))
                    dve.tensor_tensor(xl[0:C, rowcols(b, r)], ps[0:C, 4 + (G * par + r) % 2, 0:UT],
                                      xh[0:C, rowcols(b, r)], ALU.subtract).then_inc(S["xl_ready"], 1)
                dve.wait_ge(S["gate_done"], b + 1)
                raw = ps[0:PT, 6, 0:T * E].rearrange("p (t e) -> p t e", e=E)

                def over_experts(v):
                    return v.unsqueeze(2).to_broadcast([PT, T, E])

                s.link(dve.tensor_reduce(gs[:, 0, :], raw, AX.X, ALU.max))
                dve.tensor_tensor(gl[:], raw, over_experts(gs[:, 0, :]), ALU.subtract
                                  ).then_inc(S["gate_shifted"], 1)
                dve.wait_ge(S["gate_exp"], b + 1)
                s.link(dve.tensor_reduce(gs[:, 1, :], gl[:], AX.X, ALU.add))
                s.link(dve.reciprocal(gs[:, 1, :], gs[:, 1, :]))
                s.link(dve.tensor_tensor(gl[:], gl[:], over_experts(gs[:, 1, :]), ALU.mult))
                pair = gc[:].rearrange("p t (e j) -> p t e j", e=E)
                s.link(dve.tensor_tensor(pair, gl[:].unsqueeze(2).to_broadcast([PT, T, E, E]),
                                         gl[:].unsqueeze(3).to_broadcast([PT, T, E, E]), ALU.is_ge))
                s.link(dve.tensor_tensor(gc[:], gc[:], below[0:PT, :].unsqueeze(1).to_broadcast([PT, T, E * E]),
                                         ALU.mult))
                s.mark(dve.tensor_reduce(ga[:, 0, :, :], pair, AX.X, ALU.add))
                s.link(dve.tensor_reduce(ga[:, 1, :, :], gc[:].rearrange("p t (e j) -> p t j e", e=E), AX.X,
                                         ALU.add))
                s.link(dve.tensor_tensor(ga[:, 0, :, :], ga[:, 0, :, :], ga[:, 1, :, :], ALU.subtract))
                s.link(dve.tensor_tensor(ga[:, 0, :, :], ga[:, 0, :, :],
                                         rankmax[0:PT, :].unsqueeze(1).to_broadcast([PT, T, E]), ALU.is_lt))
                s.link(dve.tensor_tensor(gl[:], gl[:], ga[:, 0, :, :], ALU.mult))
                s.link(dve.tensor_reduce(gs[:, 2, :], gl[:], AX.X, ALU.add))
                s.link(dve.tensor_scalar(gs[:, 2, :], gs[:, 2, :], WS, WS * 1e-9, ALU.mult, ALU.add))
                s.link(dve.reciprocal(gs[:, 2, :], gs[:, 2, :]))
                dve.tensor_tensor(gl[:], gl[:], over_experts(gs[:, 2, :]), ALU.mult
                                  ).then_inc(S["gate_ready"], 1)
            s.image(0, 21)

            def low_part(i, e):
                dve.wait_ge(S["h_ready"], i + 2)
                dve.tensor_tensor(hl[e % 2], h32[e % 2], hh[e % 2], ALU.subtract).then_inc(S["hl_ready"], 1)

            def weigh(u, par, e):
                i = u * E + e
                if e == 0:
                    dve.wait_ge(S[f"unit_in{par}"], u * 16 + (32 - 16 * par))
                    dve.wait_ge(S[f"out_stored{par}"], u * 8 - 8 * par + 1)
                dve.wait_ge(S["y_done"], i + 3)
                dst = res[par] if e == 0 else acc[e % 2]
                dve.scalar_tensor_tensor(out=dst, in0=ps[0:C, 6 + e % 2, 0:UT], scalar=b2_sb[:, e:e + 1],
                                         in1=gb[par][:, e, :], op0=ALU.add, op1=ALU.mult
                                         ).then_inc(S["y_free"], 1)
                if e == 0:
                    dve.wait_ge(S["y_free"], i + 3)
                    dve.tensor_tensor(res[par], res[par], tb[par], ALU.add).then_inc(S["sum_ready"], 1)
                else:
                    dve.wait_ge(S["y_free"], i + 3)
                    dve.wait_ge(S["sum_ready"], u * (E - 1) + e if e > 0 else 0)
                    dve.tensor_tensor(res[par], res[par], acc[e % 2], ALU.add).then_inc(
                        S["sum_ready" if e < E - 1 else "res_ready"], 1)

            low_part(0, 0)
            with dve.Fori(0, U // 2 - 1) as pair:
                for par in range(2):
                    for e in range(E):
                        u = pair * 2 + par
                        weigh(u, par, e)
                        low_part(u * E + e + 1, (e + 1) % E)
            for par in range(2):
                for e in range(E):
                    u = U - 2 + par
                    weigh(u, par, e)
                    if (par, e) != (1, E - 1):
                        low_part(u * E + e + 1, (e + 1) % E)

        @block.tensor
        def _(pe):
            pe.wait_ge(S["consts_in"], 16 * N_CONST)
            pe.wait_ge(S["weights_ready"], 1)

            for b, par in images(pe):
                pe.wait_ge(S[f"x_in{par}"], b * 8 + (16 - 8 * par))
                for r in range(G):
                    bank = (G * par + r) % 2
                    if r >= 2:
                        pe.wait_ge(S["xT_copied"], b * G + (r - 1))
                    for j in range(TU):
                        c0 = r * UT + j * PT
                        ins = pe.transpose(ps[0:PT, bank, j * C:(j + 1) * C], xc[:, par, c0:c0 + PT],
                                           ident[0:C, 0:C])
                    ins.then_inc(S["xT_done"], 1)
                for r in range(G):
                    pe.wait_ge(S["xn_ready"], b * G + (r + 1))
                    if r >= 2:
                        pe.wait_ge(S["xnC_ready"], b * G + (r - 1))
                    for j in range(TU):
                        ins = pe.matmul(ps[0:C, 2, r * GP:(r + 1) * GP], xt[:, par, r * TU + j, 0:C],
                                        cellmean[0:PT, :], start=(j == 0), stop=(j == TU - 1))
                    if r == G - 1:
                        ins.then_inc(S["sf_done"], 1)
                    for j in range(TU):
                        ins = pe.transpose(ps[0:C, 3 + (G * par + r) % 2, j * PT:(j + 1) * PT],
                                           xt[:, par, r * TU + j, 0:C], ident[0:PT, 0:PT])
                    ins.then_inc(S["xnC_done"], 1)
                pe.wait_ge(S["sf_ready"], b + 1)
                for r in range(G):
                    pe.wait_ge(S["xnC_ready"], b * G + (r + 1))
                    for j in range(TU):
                        t = r % 4 * TU + j
                        c0 = r * UT + j * PT
                        ins = pe.matmul(ps[0:PT, 5 + r // 4, t * K9:(t + 1) * K9], xc[:, par, c0:c0 + PT],
                                        sf[:, r * GP:r * GP + K9], start=True, stop=True)
                ins.then_inc(S["logits_done"], 1)
                pe.wait_ge(S["aff_ready"], b + 1)
                pe.matmul(ps[0:CB, 7, 0:GP * GP], zeros[:], ident[0:PT, 0:GP * GP], start=True, stop=False,
                          skip_group_check=True)
                for t in range(T):
                    r = t // TU
                    ins = pe.matmul(ps[0:CB, 7, r * GP:r * GP + K9], xt[:, par, t, :], aff[:, t, :],
                                    start=False, stop=(t == T - 1), skip_group_check=True)
                ins.then_inc(S["sft_done"], 1)
                pe.wait_ge(S["aff_hi"], b * 2 + 2)
                pe.wait_ge(S["aff_lo"], b + 1)
                for r in range(G):
                    if r < 2:
                        pe.wait_ge(S["xT_copied"], b * G + G)
                    else:
                        pe.wait_ge(S["affT_ready"], b * G + (r - 1))
                    for j in range(TU):
                        ins = pe.transpose(ps[0:3 * ZONE, (G * par + r) % 2,
                                              j * PT // 2:(j + 1) * PT // 2].bitcast(F16),
                                           aff16[:, r * TU + j, :], ident16[0:PT, 0:PT])
                    ins.then_inc(S["affT_done"], 1)
                pe.wait_ge(S["sft_ready"], b + 1)
                pe.wait_ge(S["affT_ready"], b * G + G)

            for b in range(B):
                ins = pe.transpose(ps[0:N, 0, b * CB:(b + 1) * CB], sft[:, b * N:(b + 1) * N], ident[0:CB, 0:CB])
            ins.then_inc(S["attn_pe"], 1)
            pe.wait_ge(S["attn_dve"], 1)
            for b in range(B):
                ins = pe.transpose(ps[0:C, 1, b * N:(b + 1) * N], sftT[:, b, :], ident[0:N, 0:N])
            ins.then_inc(S["attn_pe"], 1)
            pe.wait_ge(S["attn_dve"], 2)
            for which in range(2):
                for h in range(HEADS):
                    w0 = which * C + h * HD
                    ins = pe.matmul(ps[0:HD, 4 * which + h // 2, h % 2 * B * N:(h % 2 + 1) * B * N],
                                    wqkv_sb[:, w0:w0 + HD], sfn[:].rearrange("p b n -> p (b n)"),
                                    start=True, stop=True)
            ins.then_inc(S["attn_pe"], 1)
            pe.wait_ge(S["attn_dve"], 3)
            for b in range(B):
                ins = pe.matmul(ps[0:N, 0, b * C:(b + 1) * C], sfn[:, b, :], wqkv_sb[:, 2 * C:3 * C],
                                start=True, stop=True)
            ins.then_inc(S["attn_pe"], 1)
            pe.wait_ge(S["attn_act"], 1)
            for b in range(B):
                for h in range(HEADS):
                    ins = pe.matmul(ps[0:N, 4 + b, h * N:(h + 1) * N], q[:, h, b * N:(b + 1) * N],
                                    k[:, h, b * N:(b + 1) * N], start=True, stop=True)
            ins.then_inc(S["attn_pe"], 1)
            pe.wait_ge(S["attn_dve"], 4)
            pe.wait_ge(S["attn_act"], 2)
            for b in range(B):
                for h in range(HEADS):
                    ins = pe.transpose(ps[0:N, b, h * N:(h + 1) * N], prob[:, b, h, :], ident[0:N, 0:N])
            ins.then_inc(S["attn_pe"], 1)
            pe.wait_ge(S["attn_dve"], 6)
            for b in range(B):
                for h in range(HEADS):
                    c0 = b * C + h * HD
                    ins = pe.matmul(ps[0:N, 4, c0:c0 + HD], probT[:, b, h, :], vT[:, b, h * HD:(h + 1) * HD],
                                    start=True, stop=True)
            ins.then_inc(S["attn_pe"], 1)
            pe.wait_ge(S["attn_dve"], 7)
            for b in range(B):
                ins = pe.transpose(ps[0:C, 5, b * N:(b + 1) * N], ao[:, b, :], ident[0:N, 0:N])
            ins.then_inc(S["attn_pe"], 1)
            pe.wait_ge(S["attn_dve"], 8)
            for u in range(U):
                b, r = divmod(u, G)
                n = BANK // C
                for zone in range(3):
                    ins = pe.matmul(ps[zone * ZONE:(zone + 1) * ZONE, u // n, u % n * C:(u % n + 1) * C],
                                    aoT[:, b, r * GP:r * GP + ZONE], wproj_sb[:], start=True, stop=True)
            ins.then_inc(S["attn_pe"], 1)
            pe.wait_ge(S["attn_dve"], 9)

            def gate_tiles(b, par, r):
                pe.wait_ge(S["xl_ready"], b * G + (r + 1))
                for j in range(TU):
                    t = r * TU + j
                    passes = ((xh, gate_hi), (xl, gate_hi), (xh, gate_lo), (xl, gate_lo))
                    for i, (xx, ww) in enumerate(passes):
                        ins = pe.matmul(ps[0:PT, 6, t * E:(t + 1) * E], xx[:, bass.ds(b * IMG + t * PT, PT)],
                                        ww[:], start=(i == 0), stop=(i == 3))
                return ins

            def transpose_mid(b, par, r):
                pe.wait_ge(S["mid_ready"], b * G + (r + 1))
                if r >= 2:
                    pe.wait_ge(S["tT_copied"], b * G + (r - 1))
                for j in range(TU):
                    c0 = r * UT + j * PT
                    ins = pe.transpose(ps[0:PT, 2 + (G * par + r) % 2, j * C:(j + 1) * C],
                                       xc[:, par, c0:c0 + PT], ident[0:C, 0:C])
                ins.then_inc(S["tT_done"], 1)

            for b, par in images(pe):
                for r in range(G):
                    if r >= 2:
                        pe.wait_ge(S["mid_ready"], b * G + (r - 1))
                    pe.matmul(ps[0:C, (G * par + r) % 2, 0:UT], so[:, b * G + r, :], affT[:, rowcols(b, r)],
                              start=True, stop=True).then_inc(S["pix_done"], 1)
                    if r >= 1:
                        transpose_mid(b, par, r - 1)
                transpose_mid(b, par, G - 1)
                for r in range(G):
                    pe.wait_ge(S["x2_ready"], b * G + (r + 1))
                    if r >= 2:
                        pe.wait_ge(S["xl_ready"], b * G + (r - 1))
                    for j in range(TU):
                        ins = pe.transpose(ps[0:C, 4 + (G * par + r) % 2, j * PT:(j + 1) * PT],
                                           xt[:, par, r * TU + j, 0:C], ident[0:PT, 0:PT])
                    ins.then_inc(S["x2C_done"], 1)
                    if r >= 1:
                        gate_tiles(b, par, r - 1)
                gate_tiles(b, par, G - 1).then_inc(S["gate_done"], 1)
                pe.wait_ge(S["gate_ready"], b + 1)
                pe.transpose(ps[0:T * E, 7, 0:PT], gl[:].rearrange("p t e -> p (t e)"), ident[0:PT, 0:PT]
                             ).then_inc(S["gT_done"], 1)
                pe.wait_ge(S["gT_copied"], b + 1)

            def first_layer(u, e):
                for c in range(CH):
                    w0 = e * HID + c * 128
                    for i, (ww, xx) in enumerate(((w1_hi, xh), (w1_hi, xl), (w1_lo, xh))):
                        ins = pe.matmul(ps[:, CH * (e % 2) + c, 0:UT], ww[:, w0:w0 + 128], xx[:, unit_cols(u)],
                                        start=(i == 0), stop=(i == 2))
                ins.then_inc(S["z_done"], 1)

            def second_layer(u, e):
                i = u * E + e
                y = ps[0:C, 6 + e % 2, 0:UT]
                pe.wait_ge(S["y_free"], i + 1)
                pe.wait_ge(S["hh_ready"], i + 1)
                for c in range(CH):
                    pe.matmul(y, w2_hi[:, e * CH + c, :], hh[e % 2][:, c, :], start=(c == 0), stop=False)
                    pe.matmul(y, w2_lo[:, e * CH + c, :], hh[e % 2][:, c, :], start=False, stop=False)
                pe.wait_ge(S["hl_ready"], i + 1)
                for c in range(CH):
                    ins = pe.matmul(y, w2_hi[:, e * CH + c, :], hl[e % 2][:, c, :], start=False,
                                    stop=(c == CH - 1))
                ins.then_inc(S["y_done"], 1)

            def unit(u, last):
                for e in range(E):
                    if e < E - 1 or not last:
                        v, f = (u, e + 1) if e < E - 1 else (u + 1, 0)
                        pe.wait_ge(S["h_ready"], u * E + e + 1)
                        first_layer(v, f)
                    second_layer(u, e)

            first_layer(0, 0)
            with pe.Fori(0, U - 1) as u:
                unit(u, False)
            unit(U - 1, True)


def kernel(x, L0_conv_xl, L0_conv_qkv_w, L0_conv_proj_w, L0_conv_proj_b, L0_ffn_gate_w, L0_ffn_gate_b, L0_ffn_w1,
           L0_ffn_b1, L0_ffn_w2, L0_ffn_b2):
    import concourse.bacc as bacc
    from concourse.bass_utils import run_bass_kernel_spmd

    def lay(a):
        return np.ascontiguousarray(np.asarray(a))

    table, inner = constants()
    wqkv = np.asarray(L0_conv_qkv_w).reshape(HEADS, 3, HD, C).transpose(3, 1, 0, 2).reshape(C, 3 * C)
    arrays = {
        "x": lay(np.asarray(x).transpose(1, 0, 2, 3).reshape(C, TOK)),
        "table": table,
        "inner": inner,
        "wqkv": lay(wqkv),
        "wproj": lay(np.asarray(L0_conv_proj_w).T),
        "bproj": lay(L0_conv_proj_b).reshape(1, C),
        "gate_w": lay(L0_ffn_gate_w),
        "gate_b": lay(L0_ffn_gate_b).reshape(1, E),
        "w1": lay(np.asarray(L0_ffn_w1).transpose(1, 0, 2).reshape(C, E * HID)),
        "b1": lay(L0_ffn_b1).reshape(1, E * HID),
        "w2": lay(np.asarray(L0_ffn_w2).reshape(E, CH, 128, C).transpose(2, 0, 1, 3).reshape(128, E * CH * C)),
        "b2": lay(np.asarray(L0_ffn_b2).T),
    }
    nc = bacc.Bacc("TRN2", target_bir_lowering=False, num_devices=1)
    args = [nc.dram_tensor(n, a.shape, mybir.dt.from_np(a.dtype), kind="ExternalInput").ap()
            for n, a in arrays.items()]
    mid = nc.dram_tensor("mid", [C, TOK], F32, kind="Internal").ap()
    gates = nc.dram_tensor("gates", [E, TOK], F32, kind="Internal").ap()
    out = nc.dram_tensor("out", [C, TOK], F32, kind="ExternalOutput").ap()
    build(nc, *args, mid, gates, out)
    r = run_bass_kernel_spmd(nc, [arrays], core_ids=[0])
    return r.results[0]["out"].reshape(C, B, H, W).transpose(1, 0, 2, 3)
```

```python
from contextlib import ExitStack

import numpy as np

import concourse.bass as bass
from concourse import mybir

F32 = mybir.dt.float32
F16 = mybir.dt.float16
ALU = mybir.AluOpType
ACT = mybir.ActivationFunctionType
AX = mybir.AxisListType

B, C, H, W = 4, 96, 56, 56
SP = 8
G = H // SP
GP = G + 2
N = G * G
K9 = 3 * GP
PT = 2 * W
TU = SP * W // PT
UT = TU * PT
U = B * G
T = G * TU
IMG = H * W
TOK = B * IMG
HEADS = 8
HD = C // HEADS
PAIRS = B // 2
HALF = 64
GROUPS = HEADS * 32 // 128
E = 4
HID = 4 * C
CH = HID // 128
CB = C + 1
WS = 64.0
BANK = 512
ZONE = 32
NEG = -1.0e30


def constants():
    p = np.arange(128)
    cell = (p % W) // SP + 1
    col = np.arange(GP)
    near = np.where(np.abs(col[None] - cell[:, None]) <= 1, 0.0, NEG)
    e = np.arange(E)
    below = np.tile((e[None, :] < e[:, None]).reshape(1, E * E), (128, 1))
    rank = np.tile((e - 1.5)[None], (128, 1))
    table = np.concatenate([np.eye(128), np.tile(near, (1, 3)), below, rank], axis=1)
    inner = np.zeros((GP, GP))
    inner[1:-1, 1:-1] = 1.0
    row = np.tile(np.concatenate([inner.reshape(-1), np.zeros(9)]), (1, B))
    return table.astype(np.float32), row.astype(np.float32)


AW = GP * GP + 9


def build(nc, x, xtok, table, inner, wqkv, wproj, bproj, gate_w, gate_b, w1, b1, w2, b2, gates, out):
    with ExitStack() as ctx:
        def sb(name, shape, dt=F32):
            return ctx.enter_context(nc.sbuf_tensor(name, shape, dt))

        def sem(name):
            return ctx.enter_context(nc.semaphore(name))

        tab = sb("tab", [128, table.shape[1]])
        o = 0
        ident = tab[:, 0:128]
        o = 128
        near = tab[:, o:o + K9]
        o += K9
        below = tab[:, o:o + E * E]
        o += E * E
        rankmax = tab[:, o:o + E]
        ident16 = sb("ident16", [128, 128], F16)
        wqkv_sb = sb("wqkv_sb", [C, 2 * HEADS * ZONE + C])
        wproj_sb = sb("wproj_sb", [CB, C])
        gate_hl = sb("gate_hl", [CB, 2 * E], F16)
        w1_hi = sb("w1_hi", [CB, E * HID], F16)
        w1_lo = sb("w1_lo", [CB, E * HID], F16)
        w2_hi = sb("w2_hi", [128, E * CH, C], F16)
        w2_lo = sb("w2_lo", [128, E * CH, C], F16)
        b2_sb = sb("b2_sb", [C, E])
        gate_st = sb("gate_st", [CB, E])

        xt = sb("xt", [PT, 2, T, CB])
        xm = xt[:, 1, :, 0:C]
        x16 = xt[:, 0, :, :].rearrange("p t c -> p (t c)").bitcast(F16)[:, 0:2 * T * C].rearrange(
            "p (t h c) -> p t h c", h=2, c=C)
        st = sb("st", [PT, T, 6])
        mom = sb("mom", [PT, 5, T])
        rstd = sb("rstd", [PT, T])
        minus_half = sb("minus_half", [PT, 1])
        sf = sb("sf", [C, GP * GP])
        sf16 = sb("sf16", [C, 2, GP * GP], F16)
        aff = sb("aff", [PT, T, K9])
        affs = sb("affs", [PT, 2, T])
        aff16 = sb("aff16", [PT, T, 3 * ZONE], F16)
        affT = sb("affT", [3 * ZONE, TOK], F16)
        sft = sb("sft", [CB, B * N])
        zeros = sb("zeros", [PT, CB])
        xnC = sb("xnC", [C, 2, IMG], F16)
        sftT = sb("sftT", [N, B, C])
        srec = sb("srec", [N, B])
        sfn = sb("sfn", [C, B, N])
        vT = sb("vT", [N, B, HEADS, HD + 1])
        peak = sb("peak", [128, PAIRS, HEADS])
        arec = sb("arec", [N, B * HEADS])
        xhl = sb("xhl", [CB, 2, TOK], F16)
        ao = sb("ao", [N, B, C])
        aoT = sb("aoT", [CB, B, AW])
        so = sb("so", [3 * ZONE, U, C], F16)
        credit = sb("credit", [1, 4])
        gl = sb("gl", [PT, T, E])
        gs = sb("gs", [PT, 4, T])
        gc = sb("gc", [PT, T, E * E])
        ga = sb("ga", [PT, 2, T, E])
        gT = sb("gT", [T * E, PT])
        STAGED = 2 * E * (HID + CH * C)
        big = sb("big", [128, max(8 * CH * UT, STAGED + 2 * T * CB)], F16)
        w1_st = big[0:CB, 0:2 * E * HID].bitcast(F32)
        w2_st = big[:, 2 * E * HID:2 * E * HID + 2 * E * CH * C].bitcast(F32)
        f32 = big[:].bitcast(F32)
        SC = HEADS * N
        prob = f32[:, 0:PAIRS * SC].rearrange("p (b h n) -> p b h n", b=PAIRS, h=HEADS)
        probT = f32[0:N, PAIRS * SC:(PAIRS + B) * SC].rearrange("p (b h n) -> p b h n", b=B, h=HEADS)
        QW = B * N + HALF - N
        q = f32[:, (PAIRS + B) * SC:(PAIRS + B) * SC + GROUPS * QW].rearrange("p (g n) -> p g n", g=GROUPS)
        k = f32[:, (PAIRS + B) * SC + GROUPS * QW:(PAIRS + B) * SC + 2 * GROUPS * QW].rearrange(
            "p (g n) -> p g n", g=GROUPS)
        images = [xt[:, 0, :, :], xt[:, 1, :, :],
                  big[0:PT, STAGED:STAGED + 2 * T * CB].bitcast(F32).rearrange("p (t c) -> p t c", c=CB)]
        HW_ = CH * UT
        h32 = [big[:, 2 * i * HW_:2 * (i + 1) * HW_].bitcast(F32).rearrange("p (c n) -> p c n", c=CH)
               for i in range(2)]
        hh = [big[:, (4 + i) * HW_:(5 + i) * HW_].rearrange("p (c n) -> p c n", c=CH) for i in range(2)]
        hl = [big[:, (6 + i) * HW_:(7 + i) * HW_].rearrange("p (c n) -> p c n", c=CH) for i in range(2)]
        gb = [sb(f"gb{i}", [C, E, UT]) for i in range(3)]
        res = [sb(f"res{i}", [C, UT]) for i in range(3)]
        acc = [sb(f"acc{i}", [C, UT]) for i in range(2)]

        ps = ctx.enter_context(nc.psum_tensor("ps", [128, 8, BANK], F32))

        names = """consts_in xa_in0 xa_in1 xa_in2 xb_in0 xb_in1 xb_in2 xm_in0 xm_in1 init_done pool_init weights_ready ident16_ready weights_step zeros_step
            moments_ready rstd_ready centred xn_ready sf_ready xnC_done
            hi_ready lo_ready grid_step logits_done shifted exp_ready aff_ready aff_hi aff_lo sft_done sft_ready affT_done affT_ready
            super_turned super_ready superT_done superT_ready qk_done q_ready k_ready v_done v_ready
            scores_done attn_step scores_shifted prob_ready probT_done probT_ready0 probT_ready1
            heads_done heads_ready headsT_done headsT_ready proj_done so_hi so_lo norm1_step norm2_step norm3_step
            side_done side_read x2_ready x2_hi x2_lo xhl_ready gate_shifted gate_exp gate_ready gT_copied gates_out
            z_done hh_ready h_ready hl_ready y_done y_read sum_done unit_in0 unit_in1 unit_in2
            out_stored0 out_stored1 out_stored2""".split()
        S = {n: sem(n) for n in names}
        N_CONST = 11
        N_POOL = 3

        CUT = 4

        def image(b):
            return images[b % 3]

        LOGITS, SUPER = (0, 1, 5, 6), 7

        def turn_order():
            for b in range(B):
                for r in range(G):
                    yield "xn", b, r
                if b > 0:
                    for r in range(G):
                        yield "aff", b - 1, r

        turns = list(turn_order())
        TURNS = 3

        def turn_bank(kind, b, r):
            if (kind, b) == ("aff", B - 1):
                return 2 + r % 2
            return 2 + turns.index((kind, b, r)) % TURNS

        def turn_before(kind, b, r):
            n = turns.index((kind, b, r))
            return turns[n - TURNS] if n >= TURNS else None

        block = ctx.enter_context(nc.Block())

        def rowcols(b, r):
            return bass.ds(b * IMG + r * UT, UT)

        SIDE, Y = 7, 6
        PIX, MEAN, SCALE, TURN, GATE, GT = 2, 9, 11, 13, 20, 26
        early = {PIX + r: ("pix", r) for r in range(G)} | {TURN + r: ("turn", r) for r in range(G)}
        early |= {GATE: ("gate", 0), GT: ("gT", 0)}
        SLOTS = G * E
        order = []
        for slot in range(SLOTS):
            if slot in early:
                order.append(early[slot])
            if slot % E == 0:
                order.append(("res", slot // E))
        alone = [v for v in order if v[0] != "res"]

        def visit(b, kind, r):
            if isinstance(b, int) and b == -1:
                return alone.index((kind, r))
            if isinstance(b, int) and b == B - 1:
                return len(alone) + (B - 1) * len(order) + r
            return b * len(order) + (len(alone) + order.index((kind, r)))

        FIRST = (SIDE, Y)
        FIRST_GATE = 3

        def probT_pair(p):
            return probT[:, 2 * p:2 * p + 2, :, :].rearrange("n b h m -> n h b m")

        def probT_psum(p):
            return ps[0:N, 4 * p:4 * p + 2, :].rearrange("n a (h b m) -> n (a h) b m", b=2, m=HALF)[:, :, :, 0:N]

        def banks_of(b):
            n = BANK // C
            first = 4 * (b % 2)
            return (first, range(0, n)), (first + 1, range(n, G))

        def buf(r):
            return r % 2 if r < G - 1 else 2

        def uses(b, r):
            return b * 3 + (r // 2 + 1) if r < G - 1 else b + 1

        @block.sync
        def _(sp):
            def load_phase1(b):
                for part, t0, t1 in (("a", 0, CUT * TU), ("b", CUT * TU, T)):
                    sp.dma_start(image(b)[:, t0:t1, :], xtok[:, b, t0:t1, :]
                                 ).then_inc(S[f"x{part}_in{b % 3}"], 16)

            load_phase1(0)
            for dst, src in ((tab[:], table), (wqkv_sb[:], wqkv), (wproj_sb[0:C, :], wproj),
                             (wproj_sb[C:CB, :], bproj), (gate_st[0:C, :], gate_w), (gate_st[C:CB, :], gate_b)):
                sp.dma_start(dst, src).then_inc(S["consts_in"], 16)
            load_phase1(1)
            for dst, src in ((w1_st[0:C, :], w1), (w1_st[C:CB, :], b1), (w2_st, w2), (b2_sb[:], b2)):
                sp.dma_start(dst, src).then_inc(S["consts_in"], 16)
            sp.wait_ge(S["init_done"], 1)
            sp.dma_start(aoT[C:CB, :, :], inner.rearrange("o (b n) -> o b n", b=B)).then_inc(S["consts_in"], 16)
            load_phase1(2)
            for b in range(3, B):
                sp.wait_ge(S["sft_done"], b - 2)
                load_phase1(b)

            def load_channels(b, r):
                k_ = buf(r)
                sp.dma_start(res[k_][:], x[:, rowcols(b, r)]).then_inc(S[f"unit_in{k_}"], 16)

            def load_gates(b, r):
                k_ = buf(r)
                sp.dma_start(gb[k_][:], gates[:, rowcols(b, r)].unsqueeze(0).to_broadcast([C, E, UT])
                             ).then_inc(S[f"unit_in{k_}"], 16)

            def load_unit(b, r):
                load_channels(b, r)
                load_gates(b, r)

            def store_unit(b, r):
                k_ = buf(r)
                sp.wait_ge(S["sum_done"], b * SLOTS + ((r + 1) * E + 2))
                sp.dma_start(out[:, rowcols(b, r)], res[k_][:]).then_inc(S[f"out_stored{k_}"], 16)
                sp.wait_ge(S[f"out_stored{k_}"], uses(b, r) * 16)

            for r in (0, 1, G - 1):
                load_channels(0, r)
            sp.wait_ge(S["gates_out"], 16)
            for r in (0, 1, G - 1):
                load_gates(0, r)
            with sp.Fori(0, B - 1) as b:
                for r in range(G):
                    store_unit(b, r)
                    if r < 4:
                        load_unit(b, r + 2)
                    else:
                        if r == 4:
                            sp.wait_ge(S["gates_out"], b * 16 + 32)
                        load_unit(b + 1, r - 4 if r < G - 1 else r)
            for r in range(G):
                store_unit(B - 1, r)
                if r < 4:
                    load_unit(B - 1, r + 2)

        @block.gpsimd
        def _(pool):
            pool.memset(minus_half[:], -0.5).then_inc(S["pool_init"], 1)
            pool.wait_ge(S["pool_init"], 1)

            def inverse_deviation(n, t0=0, t1=T):
                pool.wait_ge(S["moments_ready"], n + 1)
                pool.tensor_tensor(rstd[:, t0:t1], mom[:, 4, t0:t1], minus_half[:].to_broadcast([PT, t1 - t0]),
                                   ALU.pow).then_inc(S["rstd_ready"], 1)

            inverse_deviation(0)
            def affinities_low(b):
                pool.wait_ge(S["aff_ready"], b + 1)
                pool.wait_ge(S["aff_hi"], b * 2 + 1)
                pool.tensor_tensor(aff16[:, :, ZONE:ZONE + K9], aff[:], aff16[:, :, 0:K9],
                                   ALU.subtract).then_inc(S["aff_lo"], 1)
                pool.wait_ge(S["aff_lo"], b + 1)

            for n in range(1, B):
                inverse_deviation(n)
                for r in range(G):
                    if r == CUT:
                        pool.wait_ge(S["rstd_ready"], n + 1)
                        rest = image(n)[:, CUT * TU:T, 0:C]
                        pool.tensor_tensor(rest, rest, mom[:, 0, CUT * TU:T].unsqueeze(2).to_broadcast(
                            [PT, T - CUT * TU, C]), ALU.add).then_inc(S["centred"], 1)
                    pool.wait_ge(S["centred"], 2 * n - (1 if r < CUT else 0))
                    tokens = image(n)[:, r * TU:(r + 1) * TU, 0:C]
                    pool.wait_ge(S["rstd_ready"], n + 1)
                    pool.tensor_tensor(tokens, tokens,
                                       rstd[:, r * TU:(r + 1) * TU].unsqueeze(2).to_broadcast([PT, TU, C]),
                                       ALU.mult).then_inc(S["xn_ready"], 1)
                    pool.wait_ge(S["xn_ready"], n * G + r + 1)
                affinities_low(n - 1)
            affinities_low(B - 1)
            for n, value in enumerate((1.0, 0.0)):
                pool.memset(xhl[C:CB, n, :], value).then_inc(S["pool_init"], 1)
                pool.wait_ge(S["pool_init"], n + 2)
            inverse_deviation(B, 0, CUT * TU)
            pool.wait_ge(S["rstd_ready"], B + 1)
            inverse_deviation(B + 1, CUT * TU, T)

            def high_part(img, r):
                pool.wait_ge(S["x2_ready"], img * G + (r + 1))
                pool.tensor_tensor(x16[:, r * TU:(r + 1) * TU, 0, :], xm[:, r * TU:(r + 1) * TU, :],
                                   zeros[:, 0:C].unsqueeze(1).to_broadcast([PT, TU, C]), ALU.add
                                   ).then_inc(S["x2_hi"], 1)
                pool.wait_ge(S["x2_hi"], img * G + (r + 1))

            for r in range(G):
                high_part(0, r)

            def add_experts(b, last):
                for r in range(G):
                    for e in range(E):
                        if not last and r * E + e == MEAN:
                            inverse_deviation(b + (B + 2))
                        if not last and 0 <= r * E + e - SCALE - 1 < G:
                            high_part(b + 1, r * E + e - SCALE - 1)
                        n = b * SLOTS + (r * E + e)
                        pool.wait_ge(S["y_read"], n + 2)
                        pool.wait_ge(S["sum_done"], n + 2)
                        pool.tensor_tensor(res[buf(r)][:], res[buf(r)][:], acc[e % 2][:], ALU.add
                                           ).then_inc(S["sum_done"], 1)

            with pool.Fori(0, B - 1) as b:
                add_experts(b, False)
            add_experts(B - 1, True)

        @block.scalar
        def _(act):
            act.wait_ge(S["init_done"], 1)

            def high_part(b, r):
                act.wait_ge(S["xnC_done"], b * G + r + 1)
                act.copy(xnC[:, 0, r * UT:(r + 1) * UT], ps[0:C, turn_bank("xn", b, r), 0:UT]
                         ).then_inc(S["hi_ready"], 1)

            def affinities_turned(b):
                for r in range(G):
                    act.wait_ge(S["affT_done"], b * G + r + 1)
                    act.copy(affT[:, rowcols(b, r)], ps[0:3 * ZONE, turn_bank("aff", b, r), 0:UT // 2].bitcast(F16)
                             ).then_inc(S["affT_ready"], 1)

            for r in range(G):
                high_part(0, r)
            for b in range(B):
                if b + 1 < B:
                    high_part(b + 1, 0)
                act.wait_ge(S["shifted"], b + 1)
                act.activation(aff[:], aff[:], ACT.Exp, scale=float(C) ** -0.5 / (SP * SP)
                               ).then_inc(S["exp_ready"], 1)
                if b + 1 < B:
                    for r in range(1, G):
                        high_part(b + 1, r)
                act.wait_ge(S["aff_ready"], b + 1)
                for zone in (0, 2):
                    act.copy(aff16[:, :, zone * ZONE:zone * ZONE + K9], aff[:]).then_inc(S["aff_hi"], 1)
                if b < B - 1:
                    affinities_turned(b)

            def load_image(img):
                for part, (t0, t1) in enumerate(((0, CUT * TU), (CUT * TU, T))):
                    act.dma_start(xt[:, 1, t0:t1, :], xtok[:, bass.ds(img, 1), t0:t1, :].rearrange(
                        "p o t c -> p (o t) c")).then_inc(S[f"xm_in{part}"], 16)

            act.wait_ge(S["sft_done"], 2)
            load_image(0)

            act.wait_ge(S["qk_done"], 1)
            act.copy(k[:, :, 0:B * N], ps[:, 6, 0:GROUPS * B * N].rearrange("p (g n) -> p g n", g=GROUPS)
                     ).then_inc(S["k_ready"], 1)
            for p in range(PAIRS):
                act.wait_ge(S["scores_shifted"], p + 1)
                act.activation(prob[:, p, :, :], prob[:, p, :, :], ACT.Exp, scale=float(HD) ** -0.5
                               ).then_inc(S["prob_ready"], 1)
            act.wait_ge(S["probT_done"], 2)
            act.copy(probT_pair(1), probT_psum(1)).then_inc(S["probT_ready1"], 1)

            def projected(b):
                act.wait_ge(S["proj_done"], b + 1)
                for bank, rows in banks_of(b):
                    ins = act.copy(so[0:ZONE, b * G + rows[0]:b * G + rows[-1] + 1, :],
                                   ps[0:ZONE, bank, 0:len(rows) * C].rearrange("p (n c) -> p n c", c=C))
                ins.then_inc(S["so_hi"], 1)
                act.wait_ge(S["so_hi"], 2 * b + 1)
                act.copy(so[ZONE:2 * ZONE, b * G:(b + 1) * G, :], so[0:ZONE, b * G:(b + 1) * G, :]
                         ).then_inc(S["so_hi"], 1)

            for b in range(B - 1):
                projected(b)
            affinities_turned(B - 1)

            def gate_exponentials(img):
                act.wait_ge(S["gate_shifted"], img + 1)
                act.activation(gl[:], gl[:], ACT.Exp, scale=1.0 / WS).then_inc(S["gate_exp"], 1)

            def store_gates(n, img):
                act.wait_ge(S["side_done"], n + 1)
                act.copy(gT[:], ps[0:T * E, SIDE, 0:PT]).then_inc(S["side_read"], 1)
                act.wait_ge(S["side_read"], n + 1)
                act.dma_start(gates[:, bass.ds(img * IMG, IMG)].rearrange("e (t p) -> t e p", p=PT),
                              gT[:]).then_inc(S["gates_out"], 16)

            def side(b, slot, img):
                r = slot - TURN
                if 0 <= r < G:
                    n = visit(b, "turn", r)
                    act.wait_ge(S["side_done"], n + 1)
                    act.copy(xhl[0:C, :, rowcols(img, r)],
                             ps[0:C, SIDE, 0:UT].bitcast(F16).rearrange("p (h n) -> p h n", h=2)
                             ).then_inc(S["side_read"], 1)
                if slot == GATE + 1:
                    gate_exponentials(img)
                if slot == GT:
                    store_gates(visit(b, "gT", 0), img)

            def hidden(i, e):
                z = ps[:, CH * (e % 2):CH * (e % 2) + CH, 0:UT]
                act.wait_ge(S["z_done"], i + 1)
                act.wait_ge(S["y_done"], i)
                act.activation(hh[e % 2], z, ACT.Gelu, scale=1.0 / WS).then_inc(S["hh_ready"], 1)
                act.activation(h32[e % 2], z, ACT.Gelu, scale=1.0 / WS).then_inc(S["h_ready"], 1)

            def load_image(img):
                for part, (t0, t1) in enumerate(((0, CUT * TU), (CUT * TU, T))):
                    act.dma_start(xt[:, 1, t0:t1, :], xtok[:, bass.ds(img, 1), t0:t1, :].rearrange(
                        "p o t c -> p (o t) c")).then_inc(S[f"xm_in{part}"], 16)

            for r in range(G):
                n = visit(-1, "turn", r)
                act.wait_ge(S["side_done"], n + 1)
                act.copy(xhl[0:C, :, rowcols(0, r)],
                         ps[0:C, FIRST[n % 2], 0:UT].bitcast(F16).rearrange("p (h n) -> p h n", h=2)
                         ).then_inc(S["side_read"], 1)
            gate_exponentials(0)
            projected(B - 1)
            act.wait_ge(S["z_done"], 1)
            act.activation(hh[0], ps[:, 0:CH, 0:UT], ACT.Gelu, scale=1.0 / WS).then_inc(S["hh_ready"], 1)
            act.activation(h32[0], ps[:, 0:CH, 0:UT], ACT.Gelu, scale=1.0 / WS).then_inc(S["h_ready"], 1)
            store_gates(visit(-1, "gT", 0), 0)
            with act.Fori(0, B - 1) as b:
                act.wait_ge(S["x2_lo"], b * G + G)
                load_image(b + 1)
                for slot in range(SLOTS):
                    side(b, slot, b + 1)
                    hidden(b * SLOTS + (slot + 1), (slot + 1) % E)
            for slot in range(SLOTS - 1):
                hidden((B - 1) * SLOTS + slot + 1, (slot + 1) % E)

        @block.vector
        def _(dve):
            class Steps:

                def __init__(self, name):
                    self.sem, self.base, self.n = S[name], 0, 0

                def image(self, b, per):
                    assert self.n in (0, per), self.n
                    self.base, self.n = b * per, 0

                def mark(self, ins):
                    ins.then_inc(self.sem, 1)
                    self.n += 1

                def settle(self):
                    dve.wait_ge(self.sem, self.base + self.n)

                def link(self, ins):
                    self.mark(ins)
                    self.settle()

            s = Steps("zeros_step")
            s.mark(dve.memset(sf[:], 0.0))
            s.mark(dve.memset(sf16[:], 0.0))
            s.mark(dve.memset(zeros[:], 0.0))
            s.mark(dve.memset(aff16[:], 0.0))
            s.mark(dve.memset(so[:], 0.0))
            s.mark(dve.memset(vT[:], 1.0))
            for n, (name, start) in enumerate((("y_done", 1), ("y_read", 1), ("h_ready", 1), ("sum_done", 2))):
                dve.memset(credit[:, n:n + 1], 0.0).then_inc(S[name], start)
            s.settle()
            dve.memset(aoT[:], 0.0).then_inc(S["init_done"], 1)

            def moments(s, eps, t0=0, t1=T):
                me, mo, qe, qo = (st[:, t0:t1, i] for i in (1, 4, 2, 5))
                m = [mom[:, i, t0:t1] for i in range(5)]
                s.mark(dve.tensor_tensor(m[1], me, mo, ALU.subtract))
                s.mark(dve.tensor_tensor(m[0], me, mo, ALU.add))
                s.link(dve.tensor_tensor(m[2], qe, qo, ALU.add))
                s.mark(dve.scalar_tensor_tensor(out=m[3], in0=m[1], scalar=0.25, in1=m[1], op0=ALU.mult,
                                                op1=ALU.mult))
                s.mark(dve.tensor_scalar(m[0], m[0], -0.5, None, ALU.mult))
                s.link(dve.tensor_scalar(m[2], m[2], 1.0 / C, eps, ALU.mult, ALU.add))
                dve.tensor_tensor(m[4], m[3], m[2], ALU.add).then_inc(S["moments_ready"], 1)

            def per_token(v, t0, t1):
                return v[:, t0:t1].unsqueeze(2).to_broadcast([PT, t1 - t0, C])

            def centre(img, r0, r1):
                t0, t1 = r0 * TU, r1 * TU
                return dve.tensor_tensor(img[:, t0:t1, :], img[:, t0:t1, :], per_token(mom[:, 0, :], t0, t1),
                                         ALU.add)

            def scale(img, r, ready):
                t0, t1 = r * TU, (r + 1) * TU
                dve.tensor_tensor(img[:, t0:t1, :], img[:, t0:t1, :], per_token(rstd, t0, t1), ALU.mult
                                  ).then_inc(ready, 1)

            def split_weights():
                s = Steps("weights_step")
                dve.wait_ge(S["consts_in"], 16 * N_CONST)
                for hi, lo, src in ((gate_hl[:, 0:E], gate_hl[:, E:2 * E], gate_st[:]),
                                    (w1_hi[:], w1_lo[:], w1_st),
                                    (w2_hi[:].rearrange("p a c -> p (a c)"),
                                     w2_lo[:].rearrange("p a c -> p (a c)"), w2_st)):
                    s.link(dve.tensor_scalar(hi, src, WS, None, ALU.mult))
                    s.mark(dve.scalar_tensor_tensor(out=lo, in0=src, scalar=WS, in1=hi, op0=ALU.mult,
                                                    op1=ALU.subtract))
                s.settle()
                dve.tensor_scalar(b2_sb[:], b2_sb[:], WS, None, ALU.mult).then_inc(S["weights_ready"], 1)
                dve.wait_ge(S["weights_ready"], 1)

            s = Steps("norm1_step")

            def statistics(b):
                for part, t0, t1 in (("a", 0, CUT * TU), ("b", CUT * TU, T)):
                    dve.wait_ge(S[f"x{part}_in{b % 3}"], 16 * (b // 3 + 1))
                    for t in range(t0, t1):
                        ins = dve.bn_stats(st[:, t, :], image(b)[:, t, 0:C])
                s.link(ins)

            def moments1(b):
                if b > 0:
                    dve.wait_ge(S["xn_ready"], b * G)
                moments(s, 1e-6)

            def channels(b, r0, r1):
                for r in range(r0, r1):
                    z = ps[0:C, turn_bank("xn", b, r), 0:UT]
                    dve.wait_ge(S["hi_ready"], b * G + r + 1)
                    dve.tensor_tensor(xnC[:, 1, r * UT:(r + 1) * UT], z, xnC[:, 0, r * UT:(r + 1) * UT],
                                      ALU.subtract)
                    dve.tensor_reduce(sf[:, (r + 1) * GP + 1:(r + 1) * GP + 1 + G],
                                      z.rearrange("p (i j s) -> p j i s", i=SP, s=SP), AX.XY, ALU.add
                                      ).then_inc(S["lo_ready"], 1)

            def cells(b):
                grid = Steps("grid_step")
                grid.base = b
                dve.wait_ge(S["lo_ready"], b * G + G)
                inner_rows = slice(GP, GP * (G + 1))
                grid.link(dve.tensor_copy(sf16[:, 0, inner_rows], sf[:, inner_rows]))
                dve.tensor_tensor(sf16[:, 1, inner_rows], sf[:, inner_rows], sf16[:, 0, inner_rows], ALU.subtract
                                  ).then_inc(S["sf_ready"], 1)

            def centre1(b):
                dve.wait_ge(S["moments_ready"], b + 1)
                centre(image(b)[:, :, 0:C], 0, CUT).then_inc(S["centred"], 1)

            statistics(0)
            moments1(0)
            s.mark(centre(image(0)[:, :, 0:C], 0, G))
            statistics(1)
            dve.wait_ge(S["rstd_ready"], 1)
            for r in range(G):
                scale(image(0)[:, :, 0:C], r, S["xn_ready"])
            moments1(1)
            channels(0, 0, G)
            cells(0)
            dve.tensor_copy(ident16[:], ident).then_inc(S["ident16_ready"], 1)
            centre1(1)
            for b in range(B):
                dve.wait_ge(S["logits_done"], b + 1)
                if b > 0:
                    dve.wait_ge(S["aff_hi"], 2 * b)
                    dve.wait_ge(S["aff_lo"], b)
                for half in range(2):
                    for n, bank in enumerate(LOGITS):
                        t0, t1 = n * 2 * TU, min((n + 1) * 2 * TU, T)
                        tiles = aff[:, t0:t1, :]
                        z = ps[0:PT, bank, 0:(t1 - t0) * 2 * K9].rearrange("p (t h n) -> p t h n", h=2, n=K9)
                        s.mark(dve.tensor_tensor(
                            tiles, z[:, :, half, :],
                            near[0:PT, :].unsqueeze(1).to_broadcast([PT, t1 - t0, K9]) if half == 0 else tiles,
                            ALU.add))
                    s.settle()
                s.link(dve.tensor_reduce(affs[:, 0, :], aff[:], AX.X, ALU.max))
                dve.tensor_tensor(aff[:], aff[:], affs[:, 0, :].unsqueeze(2).to_broadcast([PT, T, K9]),
                                  ALU.subtract).then_inc(S["shifted"], 1)
                if b + 1 < B:
                    channels(b + 1, 0, 1)
                dve.wait_ge(S["exp_ready"], b + 1)
                s.link(dve.tensor_reduce(affs[:, 1, :], aff[:], AX.X, ALU.add))
                s.link(dve.reciprocal(affs[:, 1, :], affs[:, 1, :]))
                dve.tensor_tensor(aff[:], aff[:], affs[:, 1, :].unsqueeze(2).to_broadcast([PT, T, K9]),
                                  ALU.mult).then_inc(S["aff_ready"], 1)
                if b + 1 < B:
                    channels(b + 1, 1, G)
                    cells(b + 1)
                if b + 2 < B:
                    statistics(b + 2)
                    moments1(b + 2)
                    centre1(b + 2)
                if b == B - 2:
                    split_weights()
                dve.wait_ge(S["sft_done"], b + 1)
                dve.tensor_copy(sft[:, bass.ds(b * N, N)].rearrange("p (i j) -> p i j", j=G),
                                ps[0:CB, 7, 0:GP * GP].rearrange("p (i j) -> p i j", j=GP)[:, 1:G + 1, 1:G + 1]
                                ).then_inc(S["sft_ready"], 1)

            s = Steps("attn_step")
            dve.wait_ge(S["super_turned"], 1)
            sT = ps[0:N, 0, 0:B * CB].rearrange("p (b c) -> p b c", b=B)
            s.link(dve.tensor_scalar(srec[:], sT[:, :, C], 1e-12, None, ALU.add))
            s.link(dve.reciprocal(srec[:], srec[:]))
            dve.tensor_tensor(sftT[:], sT[:, :, 0:C], srec[:].unsqueeze(2).to_broadcast([N, B, C]),
                              ALU.mult).then_inc(S["super_ready"], 1)
            dve.memset(q[:, :, B * N:QW], 0.0)
            dve.wait_ge(S["superT_done"], 1)
            dve.tensor_copy(sfn[:], ps[0:C, 1, 0:B * N].rearrange("p (b n) -> p b n", b=B)
                            ).then_inc(S["superT_ready"], 1)
            dve.wait_ge(S["qk_done"], 1)
            dve.tensor_copy(q[:, :, 0:B * N], ps[:, 5, 0:GROUPS * B * N].rearrange("p (g n) -> p g n", g=GROUPS)
                            ).then_inc(S["q_ready"], 1)
            dve.wait_ge(S["v_done"], 1)
            dve.tensor_copy(vT[:, :, :, 0:HD].rearrange("n b h d -> n (b h) d"),
                            ps[0:N, 7, 0:B * C].rearrange("n (g d) -> n g d", d=HD)).then_inc(S["v_ready"], 1)
            for p in range(PAIRS):
                dve.wait_ge(S["scores_done"], p + 1)
                scores = ps[:, 4 * p:4 * p + 4, 0:GROUPS * N].rearrange("p r (g n) -> p r g n", n=N)
                top = peak[:, p, :].rearrange("p (r g) -> p r g", g=GROUPS)
                s.link(dve.tensor_reduce(top, scores, AX.X, ALU.max))
                dve.tensor_tensor(prob[:, p, :, :].rearrange("p (g r) n -> p r g n", g=GROUPS), scores,
                                  top.unsqueeze(3).to_broadcast([128, 4, GROUPS, N]), ALU.subtract
                                  ).then_inc(S["scores_shifted"], 1)
            dve.wait_ge(S["probT_done"], 1)
            dve.tensor_copy(probT_pair(0), probT_psum(0)).then_inc(S["probT_ready0"], 1)
            dve.wait_ge(S["heads_done"], 1)
            heads = ps[0:N, 2, 0:B * HEADS * (HD + 1)].rearrange("n (g d) -> n g d", d=HD + 1)
            s.link(dve.reciprocal(arec[:], heads[:, :, HD]))
            dve.tensor_tensor(ao[:].rearrange("p b (h d) -> p (b h) d", h=HEADS), heads[:, :, 0:HD],
                              arec[:].unsqueeze(2).to_broadcast([N, B * HEADS, HD]),
                              ALU.mult).then_inc(S["heads_ready"], 1)
            dve.wait_ge(S["headsT_done"], 1)
            for b in range(B):
                dve.tensor_copy(
                    aoT[0:C, b, 0:GP * GP].rearrange("p (i j) -> p i j", j=GP)[:, 1:G + 1, 1:G + 1],
                    ps[0:C, 3, b * N:(b + 1) * N].rearrange("p (i j) -> p i j", j=G)
                    ).then_inc(S["headsT_ready"], 1)

            def projected(b):
                dve.wait_ge(S["so_hi"], 2 * b + 1)
                for bank, rows in banks_of(b):
                    units = slice(b * G + rows[0], b * G + rows[-1] + 1)
                    ins = dve.tensor_tensor(so[2 * ZONE:3 * ZONE, units, :],
                                            ps[0:ZONE, bank, 0:len(rows) * C].rearrange("p (n c) -> p n c", c=C),
                                            so[0:ZONE, units, :], ALU.subtract)
                ins.then_inc(S["so_lo"], 1)

            s = Steps("norm3_step")
            PER = 24

            def add_pixels(n, r, bank):
                dve.wait_ge(S["side_done"], n + 1)
                rows = xm[:, r * TU:(r + 1) * TU, :]
                dve.tensor_tensor(rows, rows, ps[0:PT, bank, 0:TU * C].rearrange("p (t c) -> p t c", c=C),
                                  ALU.add).then_inc(S["side_read"], 1)

            def pixel_statistics(n, r):
                dve.wait_ge(S["side_read"], n + 1)
                for t in range(r * TU, (r + 1) * TU):
                    ins = dve.bn_stats(st[:, t, :], xm[:, t, :])
                return ins

            def side_first(b, slot, img):
                r = slot - PIX
                if 0 <= r < G:
                    if r == 0:
                        s.image(b, PER)
                    if r in (0, CUT):
                        dve.wait_ge(S[f"xm_in{r // CUT}"], img * 16 + 16)
                    add_pixels(visit(b, "pix", r), r, SIDE)

            def low_tokens(img, r):
                dve.wait_ge(S["x2_hi"], img * G + (r + 1))
                dve.wait_ge(S["x2_ready"], img * G + (r + 1))
                rows = slice(r * TU, (r + 1) * TU)
                dve.tensor_tensor(x16[:, rows, 1, :], xm[:, rows, :], x16[:, rows, 0, :], ALU.subtract
                                  ).then_inc(S["x2_lo"], 1)

            def side_last(b, slot, img):
                r = slot - PIX
                if 0 <= r < G:
                    ins = pixel_statistics(visit(b, "pix", r), r)
                    if r == G - 1:
                        s.link(ins)
                if slot == MEAN:
                    moments(s, 1e-5)
                    dve.wait_ge(S["moments_ready"], img + (B + 2))
                for k_, (r0, r1) in enumerate(((0, 2), (2, 4), (4, G))):
                    if slot == MEAN + k_:
                        s.mark(centre(xm, r0, r1))
                r = slot - SCALE
                if 0 <= r < G:
                    if r == 0:
                        s.settle()
                        dve.wait_ge(S["rstd_ready"], img + (B + 2))
                    scale(xm, r, S["x2_ready"])
                r = slot - SCALE - 1
                if 0 <= r < G:
                    low_tokens(img, r)
                if slot == GATE + 1:
                    gate_probabilities(img)
                if slot == GATE + 2:
                    gate_pairs()
                if slot == GATE + 3:
                    gate_ranks()
                if slot == GATE + 4:
                    gate_chosen()
                if slot == GATE + 5:
                    gate_weights()

            def over_experts(v):
                return v.unsqueeze(2).to_broadcast([PT, T, E])

            def gate_logits(n, img, bank):
                dve.wait_ge(S["side_done"], n + 1)
                dve.tensor_reduce(gl[:], ps[0:PT, bank, 0:2 * T * E].rearrange("p (t h e) -> p t e h", h=2, e=E),
                                  AX.X, ALU.add).then_inc(S["side_read"], 1)
                dve.wait_ge(S["side_read"], n + 1)
                s.link(dve.tensor_reduce(gs[:, 0, :], gl[:], AX.X, ALU.max))
                dve.tensor_tensor(gl[:], gl[:], over_experts(gs[:, 0, :]), ALU.subtract
                                  ).then_inc(S["gate_shifted"], 1)

            pair = gc[:].rearrange("p t (e j) -> p t e j", e=E)

            def gate_probabilities(img):
                dve.wait_ge(S["gate_exp"], img + 1)
                s.link(dve.tensor_reduce(gs[:, 1, :], gl[:], AX.X, ALU.add))
                s.link(dve.reciprocal(gs[:, 1, :], gs[:, 1, :]))
                s.link(dve.tensor_tensor(gl[:], gl[:], over_experts(gs[:, 1, :]), ALU.mult))

            def gate_pairs():
                s.link(dve.tensor_tensor(pair, gl[:].unsqueeze(2).to_broadcast([PT, T, E, E]),
                                         gl[:].unsqueeze(3).to_broadcast([PT, T, E, E]), ALU.is_ge))

                s.link(dve.tensor_tensor(gc[:], gc[:], below[0:PT, :].unsqueeze(1).to_broadcast([PT, T, E * E]),
                                         ALU.mult))

            def gate_ranks():
                s.mark(dve.tensor_reduce(ga[:, 0, :, :], pair, AX.X, ALU.add))
                s.link(dve.tensor_reduce(ga[:, 1, :, :], gc[:].rearrange("p t (e j) -> p t j e", e=E), AX.X,
                                         ALU.add))
                s.link(dve.tensor_tensor(ga[:, 0, :, :], ga[:, 0, :, :], ga[:, 1, :, :], ALU.subtract))

            def gate_chosen():
                s.link(dve.tensor_tensor(ga[:, 0, :, :], ga[:, 0, :, :],
                                         rankmax[0:PT, :].unsqueeze(1).to_broadcast([PT, T, E]), ALU.is_lt))
                s.link(dve.tensor_tensor(gl[:], gl[:], ga[:, 0, :, :], ALU.mult))

            def gate_weights():
                s.link(dve.tensor_reduce(gs[:, 2, :], gl[:], AX.X, ALU.add))
                s.link(dve.tensor_scalar(gs[:, 2, :], gs[:, 2, :], WS, WS * 1e-9, ALU.mult, ALU.add))
                s.link(dve.reciprocal(gs[:, 2, :], gs[:, 2, :]))
                dve.tensor_tensor(gl[:], gl[:], over_experts(gs[:, 2, :]), ALU.mult
                                  ).then_inc(S["gate_ready"], 1)

            def low_part(i, e):
                dve.wait_ge(S["h_ready"], i + 2)
                dve.tensor_tensor(hl[e % 2], h32[e % 2], hh[e % 2], ALU.subtract).then_inc(S["hl_ready"], 1)

            def residual(b, r):
                dve.wait_ge(S[f"unit_in{buf(r)}"], uses(b, r) * 32)
                dve.wait_ge(S["side_done"], visit(b, "res", r) + 1)
                dve.tensor_tensor(res[buf(r)][:], res[buf(r)][:], ps[0:C, SIDE, 0:UT], ALU.add
                                  ).then_inc(S["side_read"], 1)

            def weigh(i, r, e):
                dve.wait_ge(S["y_done"], i + 2)
                dve.wait_ge(S["sum_done"], i + 1)
                dve.scalar_tensor_tensor(out=acc[e % 2][:], in0=ps[0:C, Y, 0:UT], scalar=b2_sb[:, e:e + 1],
                                         in1=gb[buf(r)][:, e, :], op0=ALU.add, op1=ALU.mult
                                         ).then_inc(S["y_read"], 1)

            def experts(b, last):
                for slot in range(SLOTS):
                    r, e = divmod(slot, E)
                    i = b * SLOTS + slot
                    if not last:
                        side_first(b, slot, b + 1)
                    low_part(i, e)
                    if not last and slot == GATE:
                        gate_logits(visit(b, "gate", 0), b + 1, SIDE)
                    if e == 0:
                        residual(b, r)
                    if not last:
                        side_last(b, slot, b + 1)
                    weigh(i, r, e)

            steady, s = s, Steps("norm2_step")
            projected(0)
            for r in range(G):
                if r in (0, CUT):
                    dve.wait_ge(S[f"xm_in{r // CUT}"], 16)
                n = visit(-1, "pix", r)
                add_pixels(n, r, FIRST[n % 2])
                ins = pixel_statistics(n, r)
                if r == CUT - 1:
                    s.link(ins)
                    moments(s, 1e-5, 0, CUT * TU)
            s.link(ins)
            moments(s, 1e-5, CUT * TU, T)
            for part, (r0, r1) in enumerate(((0, CUT), (CUT, G))):
                dve.wait_ge(S["moments_ready"], B + 1 + part)
                s.mark(centre(xm, r0, r1))
            s.settle()
            for r in range(G):
                dve.wait_ge(S["rstd_ready"], B + 1 + r // CUT)
                scale(xm, r, S["x2_ready"])
                if r > 0:
                    low_tokens(0, r - 1)
                if r in (3, 5):
                    projected((r - 1) // 2)
            low_tokens(0, G - 1)
            gate_logits(visit(-1, "gate", 0), 0, FIRST_GATE)
            gate_probabilities(0)
            gate_pairs()
            gate_ranks()
            gate_chosen()
            gate_weights()
            projected(B - 1)
            s = steady
            with dve.Fori(0, B - 1) as b:
                experts(b, False)
            experts(B - 1, True)

        @block.tensor
        def _(pe):
            pe.wait_ge(S["consts_in"], 16 * N_CONST)

            def free_bank(kind, b, r):
                before = turn_before(kind, b, r)
                if before is not None:
                    kind0, b0, r0 = before
                    pe.wait_ge(S["lo_ready" if kind0 == "xn" else "affT_ready"], b0 * G + r0 + 1)

            def channels(b, r):
                pe.wait_ge(S["xn_ready"], b * G + r + 1)
                free_bank("xn", b, r)
                for j in range(TU):
                    ins = pe.transpose(ps[0:C, turn_bank("xn", b, r), j * PT:(j + 1) * PT],
                                       image(b)[:, r * TU + j, 0:C], ident[0:PT, 0:PT])
                ins.then_inc(S["xnC_done"], 1)

            def logits(b):
                pe.wait_ge(S["sf_ready"], b + 1)
                for r in range(G):
                    for j in range(TU):
                        t = r % 2 * TU + j
                        c0 = r * UT + j * PT
                        for half in range(2):
                            ins = pe.matmul(ps[0:PT, LOGITS[r // 2], t * 2 * K9:(t + 1) * 2 * K9],
                                            xnC[:, half, c0:c0 + PT], sf16[:, :, r * GP:r * GP + K9],
                                            start=(half == 0), stop=(half == 1))
                ins.then_inc(S["logits_done"], 1)

            def turn_affinities(b, r):
                pe.wait_ge(S["aff_hi"], b * 2 + 2)
                pe.wait_ge(S["aff_lo"], b + 1)
                pe.wait_ge(S["ident16_ready"], 1)
                for j in range(TU):
                    columns = slice(j * PT // 2, (j + 1) * PT // 2)
                    ins = pe.transpose(ps[0:3 * ZONE, turn_bank("aff", b, r), columns].bitcast(F16),
                                       aff16[:, r * TU + j, :], ident16[0:PT, 0:PT])
                ins.then_inc(S["affT_done"], 1)

            for r in range(G):
                channels(0, r)
            logits(0)
            for b in range(B):
                if b + 1 < B:
                    for r in range(TURNS + 1):
                        channels(b + 1, r)
                pe.wait_ge(S["aff_ready"], b + 1)
                if b > 0:
                    pe.wait_ge(S["sft_ready"], b)
                pe.matmul(ps[0:CB, 7, 0:GP * GP], zeros[:], ident[0:PT, 0:GP * GP], start=True, stop=False,
                          skip_group_check=True)
                for r in range(G):
                    for t in range(r * TU, (r + 1) * TU):
                        ins = pe.matmul(ps[0:CB, 7, r * GP:r * GP + K9], image(b)[:, t, :], aff[:, t, :],
                                        start=False, stop=(t == T - 1), skip_group_check=True)
                    if b + 1 < B and TURNS + 1 + r < G:
                        channels(b + 1, TURNS + 1 + r)
                ins.then_inc(S["sft_done"], 1)
                if b + 1 < B:
                    logits(b + 1)
                if b < B - 1:
                    for r in range(G):
                        free_bank("aff", b, r)
                        turn_affinities(b, r)
            pe.wait_ge(S["sft_ready"], B)
            pe.wait_ge(S["affT_ready"], (B - 1) * G)

            for b in range(B):
                ins = pe.transpose(ps[0:N, 0, b * CB:(b + 1) * CB], sft[:, b * N:(b + 1) * N], ident[0:CB, 0:CB])
            ins.then_inc(S["super_turned"], 1)
            pe.wait_ge(S["super_ready"], 1)
            for b in range(B):
                ins = pe.transpose(ps[0:C, 1, b * N:(b + 1) * N], sftT[:, b, :], ident[0:N, 0:N])
            ins.then_inc(S["superT_done"], 1)
            pe.wait_ge(S["superT_ready"], 1)
            for which in range(2):
                for g in range(GROUPS):
                    w0 = (which * GROUPS + g) * 128
                    ins = pe.matmul(ps[:, 5 + which, g * B * N:(g + 1) * B * N], wqkv_sb[:, w0:w0 + 128],
                                    sfn[:].rearrange("p b n -> p (b n)"), start=True, stop=True)
            ins.then_inc(S["qk_done"], 1)
            for b in range(B):
                ins = pe.matmul(ps[0:N, 7, b * C:(b + 1) * C], sfn[:, b, :], wqkv_sb[:, 2 * HEADS * ZONE:],
                                start=True, stop=True)
            ins.then_inc(S["v_done"], 1)
            pe.wait_ge(S["q_ready"], 1)
            pe.wait_ge(S["k_ready"], 1)
            for p in range(PAIRS):
                if p == 1:
                    pe.wait_ge(S["v_ready"], 1)
                for b in (2 * p, 2 * p + 1):
                    for h in range(HEADS):
                        g, rows = h // 4, slice(h % 4 * ZONE, h % 4 * ZONE + HD)
                        out0, c0 = b % 2 * HALF, g * N
                        ins = pe.matmul(ps[out0:out0 + HALF, 4 * p + h % 4, c0:c0 + N],
                                        q[rows, g, b * N:b * N + HALF], k[rows, g, b * N:(b + 1) * N],
                                        start=True, stop=True)
                ins.then_inc(S["scores_done"], 1)
            for p in range(PAIRS):
                pe.wait_ge(S["prob_ready"], p + 1)
                for h in range(HEADS):
                    c0 = h % 4 * 128
                    ins = pe.transpose(ps[0:N, 4 * p + h // 4, c0:c0 + 128], prob[:, p, h, :], ident)
                ins.then_inc(S["probT_done"], 1)
            for p in range(PAIRS):
                pe.wait_ge(S[f"probT_ready{p}"], 1)
                for b in (2 * p, 2 * p + 1):
                    for h in range(HEADS):
                        c0 = (b * HEADS + h) * (HD + 1)
                        ins = pe.matmul(ps[0:N, 2, c0:c0 + HD + 1], probT[:, b, h, :], vT[:, b, h, :],
                                        start=True, stop=True)
            ins.then_inc(S["heads_done"], 1)
            pe.wait_ge(S["heads_ready"], 1)
            for b in range(B):
                ins = pe.transpose(ps[0:C, 3, b * N:(b + 1) * N], ao[:, b, :], ident[0:N, 0:N])
            ins.then_inc(S["headsT_done"], 1)

            def project(b):
                pe.wait_ge(S["headsT_ready"], b + 1)
                if b >= 2:
                    pe.wait_ge(S["so_lo"], b - 1)
                for bank, rows in banks_of(b):
                    for n, r in enumerate(rows):
                        ins = pe.matmul(ps[0:ZONE, bank, n * C:(n + 1) * C], aoT[:, b, r * GP:r * GP + ZONE],
                                        wproj_sb[:], start=True, stop=True)
                ins.then_inc(S["proj_done"], 1)

            project(0)

            def pixels(img, r, bank):
                for j in range(TU):
                    ins = pe.matmul(ps[0:PT, bank, j * C:(j + 1) * C],
                                    affT[:, bass.ds(img * IMG + (r * UT + j * PT), PT)],
                                    so[:, bass.ds(img * G + r, 1), :].rearrange("p o c -> p (o c)"),
                                    start=True, stop=True)
                return ins

            def turn(img, r, bank):
                pe.wait_ge(S["x2_hi"], img * G + (r + 1))
                pe.wait_ge(S["x2_lo"], img * G + (r + 1))
                for half in range(2):
                    for j in range(TU):
                        c0 = (half * UT + j * PT) // 2
                        ins = pe.transpose(ps[0:C, bank, c0:c0 + PT // 2].bitcast(F16),
                                           x16[:, r * TU + j, half, :], ident16[0:PT, 0:PT])
                return ins

            def gate(img, r, bank):
                for t in range(r * TU, (r + 1) * TU):
                    for half in range(2):
                        ins = pe.matmul(ps[0:PT, bank, t * 2 * E:(t + 1) * 2 * E],
                                        xhl[:, half, bass.ds(img * IMG + t * PT, PT)], gate_hl[:],
                                        start=(half == 0), stop=(half == 1))
                return ins

            def turn_gates(img):
                pe.wait_ge(S["gate_ready"], img + 1)
                return pe.transpose(ps[0:T * E, SIDE, 0:PT], gl[:].rearrange("p t e -> p (t e)"),
                                    ident[0:PT, 0:PT])

            def side(b, slot, img):
                if slot not in early:
                    return
                kind, r = early[slot]
                n = visit(b, kind, r)
                pe.wait_ge(S["side_read"], n)
                if kind == "pix":
                    ins = pixels(img, r, SIDE)
                elif kind == "turn":
                    ins = turn(img, r, SIDE)
                elif kind == "gate":
                    for unit in range(G):
                        ins = gate(img, unit, SIDE)
                else:
                    ins = turn_gates(img)
                ins.then_inc(S["side_done"], 1)

            def residual(b, r):
                pe.wait_ge(S["side_read"], visit(b, "res", r))
                pe.matmul(ps[0:C, SIDE, 0:UT], so[:, bass.ds(b * G + r, 1), :].rearrange("p o c -> p (o c)"),
                          affT[:, rowcols(b, r)], start=True, stop=True).then_inc(S["side_done"], 1)

            def first_layer(b, r, e):
                for c in range(CH):
                    w0 = e * HID + c * 128
                    for n, (ww, half) in enumerate(((w1_hi, 0), (w1_hi, 1), (w1_lo, 0))):
                        ins = pe.matmul(ps[:, CH * (e % 2) + c, 0:UT], ww[:, w0:w0 + 128],
                                        xhl[:, half, rowcols(b, r)], start=(n == 0), stop=(n == 2))
                ins.then_inc(S["z_done"], 1)

            def second_layer(i, e):
                y = ps[0:C, Y, 0:UT]
                pe.wait_ge(S["y_read"], i + 1)
                pe.wait_ge(S["hh_ready"], i + 1)
                for c in range(CH):
                    pe.matmul(y, w2_hi[:, e * CH + c, :], hh[e % 2][:, c, :], start=(c == 0), stop=False)
                    pe.matmul(y, w2_lo[:, e * CH + c, :], hh[e % 2][:, c, :], start=False, stop=False)
                pe.wait_ge(S["hl_ready"], i + 1)
                for c in range(CH):
                    ins = pe.matmul(y, w2_hi[:, e * CH + c, :], hl[e % 2][:, c, :], start=False,
                                    stop=(c == CH - 1))
                ins.then_inc(S["y_done"], 1)

            def experts(b, last):
                for slot in range(SLOTS):
                    r, e = divmod(slot, E)
                    i = b * SLOTS + slot
                    if not last:
                        side(b, slot, b + 1)
                    if not last or slot < SLOTS - 1:
                        pe.wait_ge(S["h_ready"], i + 1)
                        r1, e1 = divmod(slot + 1, E)
                        first_layer(b if r1 < G else b + 1, r1 % G, e1)
                    if e == 0:
                        residual(b, r)
                    second_layer(i, e)

            pe.wait_ge(S["so_lo"], 1)
            pe.wait_ge(S["so_hi"], 2)
            for r in range(G):
                n = visit(-1, "pix", r)
                if n >= 2:
                    pe.wait_ge(S["side_read"], n - 1)
                pixels(0, r, FIRST[n % 2]).then_inc(S["side_done"], 1)
            for b in range(1, B - 1):
                project(b)
            for r in range(G):
                if r >= 2:
                    pe.wait_ge(S["affT_ready"], (B - 1) * G + r - 1)
                turn_affinities(B - 1, r)
            pe.wait_ge(S["pool_init"], N_POOL)
            pe.wait_ge(S["weights_ready"], 1)
            for r in range(G):
                n = visit(-1, "turn", r)
                pe.wait_ge(S["side_read"], n - 1)
                if r == 1:
                    pe.wait_ge(S["affT_ready"], B * G)
                turn(0, r, FIRST[n % 2]).then_inc(S["side_done"], 1)
                if r > 0:
                    pe.wait_ge(S["side_read"], n)
                    gate(0, r - 1, FIRST_GATE)
            pe.wait_ge(S["side_read"], n + 1)
            gate(0, G - 1, FIRST_GATE).then_inc(S["side_done"], 1)
            project(B - 1)
            pe.wait_ge(S["so_lo"], B - 1)
            first_layer(0, 0, 0)
            turn_gates(0).then_inc(S["side_done"], 1)
            pe.wait_ge(S["so_lo"], B)
            pe.wait_ge(S["so_hi"], 2 * B)
            with pe.Fori(0, B - 1) as b:
                experts(b, False)
            experts(B - 1, True)


def kernel(x, L0_conv_xl, L0_conv_qkv_w, L0_conv_proj_w, L0_conv_proj_b, L0_ffn_gate_w, L0_ffn_gate_b, L0_ffn_w1,
           L0_ffn_b1, L0_ffn_w2, L0_ffn_b2):
    import concourse.bacc as bacc
    from concourse.bass_utils import run_bass_kernel_spmd

    def lay(a):
        return np.ascontiguousarray(np.asarray(a))

    table, inner = constants()
    wqkv = np.asarray(L0_conv_qkv_w).reshape(HEADS, 3, HD, C).transpose(3, 1, 0, 2)
    wqk = np.zeros((C, 2, HEADS, ZONE), np.float32)
    wqk[:, :, :, 0:HD] = wqkv[:, 0:2]
    wqkv = np.concatenate([wqk.reshape(C, -1), wqkv[:, 2].reshape(C, C)], axis=1)
    arrays = {
        "x": lay(np.asarray(x).transpose(1, 0, 2, 3).reshape(C, TOK)),
        "xtok": lay(np.concatenate([np.asarray(x).reshape(B, C, T, PT).transpose(3, 0, 2, 1),
                                    np.ones((PT, B, T, 1), np.float32)], axis=3)),
        "table": table,
        "inner": inner,
        "wqkv": lay(wqkv),
        "wproj": lay(np.asarray(L0_conv_proj_w).T),
        "bproj": lay(L0_conv_proj_b).reshape(1, C),
        "gate_w": lay(L0_ffn_gate_w),
        "gate_b": lay(L0_ffn_gate_b).reshape(1, E),
        "w1": lay(np.asarray(L0_ffn_w1).transpose(1, 0, 2).reshape(C, E * HID)),
        "b1": lay(L0_ffn_b1).reshape(1, E * HID),
        "w2": lay(np.asarray(L0_ffn_w2).reshape(E, CH, 128, C).transpose(2, 0, 1, 3).reshape(128, E * CH * C)),
        "b2": lay(np.asarray(L0_ffn_b2).T),
    }
    nc = bacc.Bacc("TRN2", target_bir_lowering=False, num_devices=1)
    args = [nc.dram_tensor(n, a.shape, mybir.dt.from_np(a.dtype), kind="ExternalInput").ap()
            for n, a in arrays.items()]
    gates = nc.dram_tensor("gates", [E, TOK], F32, kind="Internal").ap()
    out = nc.dram_tensor("out", [C, TOK], F32, kind="ExternalOutput").ap()
    build(nc, *args, gates, out)
    r = run_bass_kernel_spmd(nc, [arrays], core_ids=[0])
    return r.results[0]["out"].reshape(C, B, H, W).transpose(1, 0, 2, 3)
```

```python
from contextlib import ExitStack

import numpy as np

import concourse.bass as bass
from concourse import mybir

F32 = mybir.dt.float32
F16 = mybir.dt.float16
ALU = mybir.AluOpType
ACT = mybir.ActivationFunctionType
AX = mybir.AxisListType

B, C, H, W = 4, 96, 56, 56
SP = 8
G = H // SP
GP = G + 2
N = G * G
K9 = 3 * GP
PT = 2 * W
TU = SP * W // PT
UT = TU * PT
U = B * G
T = G * TU
IMG = H * W
TOK = B * IMG
HEADS = 8
HD = C // HEADS
PAIRS = B // 2
HALF = 64
ZONE = 32
GROUPS = HEADS * ZONE // 128
E = 4
HID = 4 * C
CH = HID // 128
CB = C + 1
WS = 64.0
BANK = 512
NEG = -1.0e30
AW = GP * GP + GP


def constants():
    p = np.arange(128)
    cell = (p % W) // SP + 1
    col = np.arange(GP)
    near = np.where(np.abs(col[None] - cell[:, None]) <= 1, 0.0, NEG)
    e = np.arange(E)
    below = np.tile((e[None, :] < e[:, None]).reshape(1, E * E), (128, 1))
    rank = np.tile((e - 1.5)[None], (128, 1))
    table = np.concatenate([np.eye(128), np.tile(near, (1, 3)), below, rank], axis=1)
    inner = np.zeros((GP, GP))
    inner[1:-1, 1:-1] = 1.0
    row = np.tile(np.concatenate([inner.reshape(-1), np.zeros(AW - GP * GP)]), (1, B))
    return table.astype(np.float32), row.astype(np.float32)



def build(nc, x, xtok, table, inner, wqkv, wproj, bproj, gate_w, gate_b, w1, b1, w2, b2, gates, out):
    with ExitStack() as ctx:
        def sb(name, shape, dt=F32):
            return ctx.enter_context(nc.sbuf_tensor(name, shape, dt))

        def sem(name):
            return ctx.enter_context(nc.semaphore(name))

        tab = sb("tab", [128, table.shape[1]])
        ident = tab[:, 0:128]
        near = tab[:, 128:128 + K9]
        below = tab[:, 128 + K9:128 + K9 + E * E]
        rankmax = tab[:, 128 + K9 + E * E:128 + K9 + E * E + E]
        ident16 = sb("ident16", [128, 128], F16)
        wqkv_sb = sb("wqkv_sb", [C, 2 * HEADS * ZONE + C])
        wproj_sb = sb("wproj_sb", [CB, C])
        gate_hl = sb("gate_hl", [CB, 2 * E], F16)
        w1_hi = sb("w1_hi", [CB, E * HID], F16)
        w1_lo = sb("w1_lo", [CB, E * HID], F16)
        w2_hi = sb("w2_hi", [128, E * CH, C], F16)
        w2_lo = sb("w2_lo", [128, E * CH, C], F16)
        b2_sb = sb("b2_sb", [C, E])
        gate_st = sb("gate_st", [CB, E])

        xt = sb("xt", [PT, 2, T, CB])
        xm = xt[:, 1, :, 0:C]
        x16 = xt[:, 0, :, :].rearrange("p t c -> p (t c)").bitcast(F16)[:, 0:2 * T * C].rearrange(
            "p (t h c) -> p t h c", h=2, c=C)
        st = sb("st", [PT, T, 6])
        mom = sb("mom", [PT, 5, T])
        rstd = sb("rstd", [PT, T])
        minus_half = sb("minus_half", [PT, 1])
        sf = sb("sf", [C, GP * GP])
        sf16 = sb("sf16", [C, 2, GP * GP], F16)
        aff = sb("aff", [PT, T, K9])
        affs = sb("affs", [PT, 2, T])
        aff16 = sb("aff16", [PT, T, 3 * ZONE], F16)
        affT = sb("affT", [3 * ZONE, TOK], F16)
        sft = sb("sft", [CB, B * N])
        zeros = sb("zeros", [PT, CB])
        xnC = sb("xnC", [C, 2, IMG], F16)
        sftT = sb("sftT", [N, B, C])
        srec = sb("srec", [N, B])
        sfn = sb("sfn", [C, B, N])
        vT = sb("vT", [N, B, HEADS, HD + 1])
        peak = sb("peak", [128, PAIRS, HEADS])
        arec = sb("arec", [N, B * HEADS])
        xhl = sb("xhl", [CB, 2, TOK], F16)
        ao = sb("ao", [N, B, C])
        aoT = sb("aoT", [CB, B, AW])
        so = sb("so", [3 * ZONE, U, C], F16)
        credit = sb("credit", [1, 4])
        gl = sb("gl", [PT, T, E])
        gs = sb("gs", [PT, 3, T])
        gc = sb("gc", [PT, T, E * E])
        ga = sb("ga", [PT, 2, T, E])
        gT = sb("gT", [T * E, PT])
        STAGED = 2 * E * (HID + CH * C)
        big = sb("big", [128, max(8 * CH * UT, STAGED + 2 * T * CB)], F16)
        w1_st = big[0:CB, 0:2 * E * HID].bitcast(F32)
        w2_st = big[:, 2 * E * HID:2 * E * HID + 2 * E * CH * C].bitcast(F32)
        big32 = big[:].bitcast(F32)
        SC = HEADS * N
        prob = big32[:, 0:PAIRS * SC].rearrange("p (b h n) -> p b h n", b=PAIRS, h=HEADS)
        probT = big32[0:N, PAIRS * SC:(PAIRS + B) * SC].rearrange("p (b h n) -> p b h n", b=B, h=HEADS)
        QW = B * N + HALF - N
        q = big32[:, (PAIRS + B) * SC:(PAIRS + B) * SC + GROUPS * QW].rearrange("p (g n) -> p g n", g=GROUPS)
        k = big32[:, (PAIRS + B) * SC + GROUPS * QW:(PAIRS + B) * SC + 2 * GROUPS * QW].rearrange(
            "p (g n) -> p g n", g=GROUPS)
        images = [xt[:, 0, :, :], xt[:, 1, :, :],
                  big[0:PT, STAGED:STAGED + 2 * T * CB].bitcast(F32).rearrange("p (t c) -> p t c", c=CB)]
        HIDW = CH * UT
        h32 = [big[:, 2 * i * HIDW:2 * (i + 1) * HIDW].bitcast(F32).rearrange("p (c n) -> p c n", c=CH)
               for i in range(2)]
        hh = [big[:, (4 + i) * HIDW:(5 + i) * HIDW].rearrange("p (c n) -> p c n", c=CH) for i in range(2)]
        hl = [big[:, (6 + i) * HIDW:(7 + i) * HIDW].rearrange("p (c n) -> p c n", c=CH) for i in range(2)]
        gb = [sb(f"gb{i}", [C, E, UT]) for i in range(3)]
        res = [sb(f"res{i}", [C, UT]) for i in range(3)]
        acc = [sb(f"acc{i}", [C, UT]) for i in range(2)]

        ps = ctx.enter_context(nc.psum_tensor("ps", [128, 8, BANK], F32))

        names = """
            consts_in xa_in0 xa_in1 xa_in2 xb_in0 xb_in1 xb_in2 xm_in0 xm_in1
            init_done pool_init weights_ready ident16_ready weights_step zeros_step
            moments_ready rstd_ready centred xn_ready sf_ready xnC_done hi_ready lo_ready grid_step
            logits_done shifted exp_ready aff_ready aff_hi aff_lo sft_done sft_ready affT_done affT_ready
            super_turned super_ready superT_done superT_ready qk_done q_ready k_ready v_done v_ready
            scores_done attn_step scores_shifted prob_ready probT_done probT_ready0 probT_ready1
            heads_done heads_ready headsT_done headsT_ready proj_done so_hi so_lo
            norm1_step norm2_step norm3_step side_done side_read x2_ready x2_hi x2_lo
            gate_shifted gate_exp gate_ready gates_out
            z_done hh_ready h_ready hl_ready y_done y_read sum_done
            unit_in0 unit_in1 unit_in2 out_stored0 out_stored1 out_stored2""".split()
        S = {n: sem(n) for n in names}
        N_CONST = 11
        N_POOL = 3
        N_INIT = 4

        CUT = 4

        def image(b):
            return images[b % 3]

        LOGITS, SUPER = (0, 1, 5, 6), 7
        VALUES = 7

        def turn_order():
            for b in range(B):
                for r in range(G):
                    yield "xn", b, r
                if b > 0:
                    for r in range(G):
                        yield "aff", b - 1, r

        turns = list(turn_order())
        TURNS = 3

        def turn_bank(kind, b, r):
            if (kind, b) == ("aff", B - 1):
                return (6, 4)[r % 2]
            return 2 + turns.index((kind, b, r)) % TURNS

        def turn_before(kind, b, r):
            n = turns.index((kind, b, r))
            return turns[n - TURNS] if n >= TURNS else None

        block = ctx.enter_context(nc.Block())

        def rowcols(b, r):
            return bass.ds(b * IMG + r * UT, UT)

        SIDE, Y = 7, 6
        PIX, MEAN, SCALE, TURN, GATE, GT = 2, 9, 11, 13, 20, 26
        early = {PIX + r: ("pix", r) for r in range(G)} | {TURN + r: ("turn", r) for r in range(G)}
        early |= {GATE: ("gate", 0), GT: ("gT", 0)}
        SLOTS = G * E
        order = []
        for slot in range(SLOTS):
            if slot in early:
                order.append(early[slot])
            if slot % E == 0:
                order.append(("res", slot // E))
        alone = [v for v in order if v[0] != "res"]

        def visit(b, kind, r):
            if isinstance(b, int) and b == -1:
                return alone.index((kind, r))
            if isinstance(b, int) and b == B - 1:
                return len(alone) + (B - 1) * len(order) + r
            return b * len(order) + (len(alone) + order.index((kind, r)))

        FIRST = (SIDE, Y)
        FIRST_GATE = 3

        def probT_pair(p):
            return probT[:, 2 * p:2 * p + 2, :, :].rearrange("n b h m -> n h b m")

        def probT_psum():
            return ps[0:N, 0:2, :].rearrange("n a (h b m) -> n (a h) b m", b=2, m=HALF)[:, :, :, 0:N]

        def banks_of(b):
            n = BANK // C
            first = (4, 4, 0, 4)[b]
            return (first, range(0, n)), (first + 1, range(n, G))

        def buf(r):
            return r % 2 if r < G - 1 else 2

        def uses(b, r):
            return b * 3 + (r // 2 + 1) if r < G - 1 else b + 1

        @block.sync
        def _(sp):
            def load_phase1(b):
                for part, t0, t1 in (("a", 0, CUT * TU), ("b", CUT * TU, T)):
                    sp.dma_start(image(b)[:, t0:t1, :], xtok[:, b, t0:t1, :]
                                 ).then_inc(S[f"x{part}_in{b % 3}"], 16)

            load_phase1(0)
            for dst, src in ((tab[:], table), (wqkv_sb[:], wqkv), (wproj_sb[0:C, :], wproj),
                             (wproj_sb[C:CB, :], bproj), (gate_st[0:C, :], gate_w), (gate_st[C:CB, :], gate_b)):
                sp.dma_start(dst, src).then_inc(S["consts_in"], 16)
            load_phase1(1)
            for dst, src in ((w1_st[0:C, :], w1), (w1_st[C:CB, :], b1), (w2_st, w2), (b2_sb[:], b2)):
                sp.dma_start(dst, src).then_inc(S["consts_in"], 16)
            sp.wait_ge(S["init_done"], 2)
            sp.dma_start(aoT[C:CB, :, :], inner.rearrange("o (b n) -> o b n", b=B)).then_inc(S["consts_in"], 16)
            load_phase1(2)
            for b in range(3, B):
                sp.wait_ge(S["sft_done"], b - 2)
                load_phase1(b)

            def load_channels(b, r):
                which = buf(r)
                sp.dma_start(res[which][:], x[:, rowcols(b, r)]).then_inc(S[f"unit_in{which}"], 16)

            def load_gates(b, r):
                which = buf(r)
                sp.dma_start(gb[which][:], gates[:, rowcols(b, r)].unsqueeze(0).to_broadcast([C, E, UT])
                             ).then_inc(S[f"unit_in{which}"], 16)

            def load_unit(b, r):
                load_channels(b, r)
                load_gates(b, r)

            def store_unit(b, r):
                which = buf(r)
                sp.wait_ge(S["sum_done"], b * SLOTS + ((r + 1) * E + 2))
                sp.dma_start(out[:, rowcols(b, r)], res[which][:]).then_inc(S[f"out_stored{which}"], 16)
                sp.wait_ge(S[f"out_stored{which}"], uses(b, r) * 16)

            for r in (0, 1, G - 1):
                load_channels(0, r)
            sp.wait_ge(S["gates_out"], 16)
            for r in (0, 1, G - 1):
                load_gates(0, r)
            with sp.Fori(0, B - 1) as b:
                for r in range(G):
                    store_unit(b, r)
                    if r < 4:
                        load_unit(b, r + 2)
                    else:
                        if r == 4:
                            sp.wait_ge(S["gates_out"], b * 16 + 32)
                        load_unit(b + 1, r - 4 if r < G - 1 else r)
            for r in range(G):
                store_unit(B - 1, r)
                if r < 4:
                    load_unit(B - 1, r + 2)

        @block.gpsimd
        def _(pool):
            pool.memset(minus_half[:], -0.5).then_inc(S["pool_init"], 1)
            pool.wait_ge(S["pool_init"], 1)
            for n, (what, value) in enumerate(((aff16, 0.0), (aoT, 0.0), (so, 0.0), (vT, 1.0))):
                pool.memset(what[:], value).then_inc(S["init_done"], 1)
                pool.wait_ge(S["init_done"], n + 1)

            def inverse_deviation(n, t0=0, t1=T):
                pool.wait_ge(S["moments_ready"], n + 1)
                pool.tensor_tensor(rstd[:, t0:t1], mom[:, 4, t0:t1], minus_half[:].to_broadcast([PT, t1 - t0]),
                                   ALU.pow).then_inc(S["rstd_ready"], 1)

            def affinities_low(b):
                pool.wait_ge(S["aff_ready"], b + 1)
                pool.wait_ge(S["aff_hi"], b * 2 + 1)
                pool.tensor_tensor(aff16[:, :, ZONE:ZONE + K9], aff[:], aff16[:, :, 0:K9],
                                   ALU.subtract).then_inc(S["aff_lo"], 1)
                pool.wait_ge(S["aff_lo"], b + 1)

            inverse_deviation(0)
            for n in range(1, B):
                inverse_deviation(n)
                for r in range(G):
                    if r == CUT:
                        pool.wait_ge(S["rstd_ready"], n + 1)
                        rest = image(n)[:, CUT * TU:T, 0:C]
                        pool.tensor_tensor(rest, rest, mom[:, 0, CUT * TU:T].unsqueeze(2).to_broadcast(
                            [PT, T - CUT * TU, C]), ALU.add).then_inc(S["centred"], 1)
                    pool.wait_ge(S["centred"], 2 * n - (1 if r < CUT else 0))
                    tokens = image(n)[:, r * TU:(r + 1) * TU, 0:C]
                    pool.wait_ge(S["rstd_ready"], n + 1)
                    pool.tensor_tensor(tokens, tokens,
                                       rstd[:, r * TU:(r + 1) * TU].unsqueeze(2).to_broadcast([PT, TU, C]),
                                       ALU.mult).then_inc(S["xn_ready"], 1)
                    pool.wait_ge(S["xn_ready"], n * G + r + 1)
                affinities_low(n - 1)
            affinities_low(B - 1)
            for n, value in enumerate((1.0, 0.0)):
                pool.memset(xhl[C:CB, n, :], value).then_inc(S["pool_init"], 1)
                pool.wait_ge(S["pool_init"], n + 2)
            inverse_deviation(B, 0, CUT * TU)
            pool.wait_ge(S["rstd_ready"], B + 1)
            inverse_deviation(B + 1, CUT * TU, T)

            def high_part(img, r):
                pool.wait_ge(S["x2_ready"], img * G + (r + 1))
                pool.tensor_tensor(x16[:, r * TU:(r + 1) * TU, 0, :], xm[:, r * TU:(r + 1) * TU, :],
                                   zeros[:, 0:C].unsqueeze(1).to_broadcast([PT, TU, C]), ALU.add
                                   ).then_inc(S["x2_hi"], 1)
                pool.wait_ge(S["x2_hi"], img * G + (r + 1))

            for r in range(G):
                high_part(0, r)

            def add_experts(b, last):
                for r in range(G):
                    for e in range(E):
                        if not last and r * E + e == MEAN:
                            inverse_deviation(b + (B + 2))
                        if not last and 0 <= r * E + e - SCALE - 1 < G:
                            high_part(b + 1, r * E + e - SCALE - 1)
                        n = b * SLOTS + (r * E + e)
                        pool.wait_ge(S["y_read"], n + 2)
                        pool.wait_ge(S["sum_done"], n + 2)
                        pool.tensor_tensor(res[buf(r)][:], res[buf(r)][:], acc[e % 2][:], ALU.add
                                           ).then_inc(S["sum_done"], 1)

            with pool.Fori(0, B - 1) as b:
                add_experts(b, False)
            add_experts(B - 1, True)

        @block.scalar
        def _(act):
            act.wait_ge(S["init_done"], N_INIT)

            def high_part(b, r):
                act.wait_ge(S["xnC_done"], b * G + r + 1)
                act.copy(xnC[:, 0, r * UT:(r + 1) * UT], ps[0:C, turn_bank("xn", b, r), 0:UT]
                         ).then_inc(S["hi_ready"], 1)

            def affinities_turned(b, r0=0, r1=G):
                for r in range(r0, r1):
                    act.wait_ge(S["affT_done"], b * G + r + 1)
                    act.copy(affT[:, rowcols(b, r)], ps[0:3 * ZONE, turn_bank("aff", b, r), 0:UT // 2].bitcast(F16)
                             ).then_inc(S["affT_ready"], 1)

            for r in range(G):
                high_part(0, r)
            for b in range(B):
                if b + 1 < B:
                    high_part(b + 1, 0)
                act.wait_ge(S["shifted"], b + 1)
                act.activation(aff[:], aff[:], ACT.Exp, scale=float(C) ** -0.5 / (SP * SP)
                               ).then_inc(S["exp_ready"], 1)
                if b + 1 < B:
                    for r in range(1, G):
                        high_part(b + 1, r)
                act.wait_ge(S["aff_ready"], b + 1)
                for zone in (0, 2):
                    act.copy(aff16[:, :, zone * ZONE:zone * ZONE + K9], aff[:]).then_inc(S["aff_hi"], 1)
                if b < B - 1:
                    affinities_turned(b)

            def load_image(img):
                for part, (t0, t1) in enumerate(((0, CUT * TU), (CUT * TU, T))):
                    act.dma_start(xt[:, 1, t0:t1, :], xtok[:, bass.ds(img, 1), t0:t1, :].rearrange(
                        "p o t c -> p (o t) c")).then_inc(S[f"xm_in{part}"], 16)

            act.wait_ge(S["sft_done"], 2)
            load_image(0)

            act.wait_ge(S["qk_done"], 1)
            act.copy(k[:, :, 0:B * N], ps[:, 6, 0:GROUPS * B * N].rearrange("p (g n) -> p g n", g=GROUPS)
                     ).then_inc(S["k_ready"], 1)

            def attention_exponentials(p):
                act.wait_ge(S["scores_shifted"], p + 1)
                act.activation(prob[:, p, :, :], prob[:, p, :, :], ACT.Exp, scale=float(HD) ** -0.5
                               ).then_inc(S["prob_ready"], 1)

            affinities_turned(B - 1, 0, 2)
            attention_exponentials(0)
            affinities_turned(B - 1, 2, G)

            def projected(b):
                act.wait_ge(S["proj_done"], b + 1)
                for bank, rows in banks_of(b):
                    ins = act.copy(so[0:ZONE, b * G + rows[0]:b * G + rows[-1] + 1, :],
                                   ps[0:ZONE, bank, 0:len(rows) * C].rearrange("p (n c) -> p n c", c=C))
                ins.then_inc(S["so_hi"], 1)
                act.wait_ge(S["so_hi"], 2 * b + 1)
                act.copy(so[ZONE:2 * ZONE, b * G:(b + 1) * G, :], so[0:ZONE, b * G:(b + 1) * G, :]
                         ).then_inc(S["so_hi"], 1)

            projected(0)
            attention_exponentials(1)
            act.wait_ge(S["probT_done"], 2)
            act.copy(probT_pair(1), probT_psum()).then_inc(S["probT_ready1"], 1)
            for b in range(1, B - 1):
                projected(b)

            def gate_exponentials(img):
                act.wait_ge(S["gate_shifted"], img + 1)
                act.activation(gl[:], gl[:], ACT.Exp, scale=1.0 / WS).then_inc(S["gate_exp"], 1)

            def store_gates(n, img):
                act.wait_ge(S["side_done"], n + 1)
                act.copy(gT[:], ps[0:T * E, SIDE, 0:PT]).then_inc(S["side_read"], 1)
                act.wait_ge(S["side_read"], n + 1)
                act.dma_start(gates[:, bass.ds(img * IMG, IMG)].rearrange("e (t p) -> t e p", p=PT),
                              gT[:]).then_inc(S["gates_out"], 16)

            def side(b, slot, img):
                r = slot - TURN
                if 0 <= r < G:
                    n = visit(b, "turn", r)
                    act.wait_ge(S["side_done"], n + 1)
                    act.copy(xhl[0:C, :, rowcols(img, r)],
                             ps[0:C, SIDE, 0:UT].bitcast(F16).rearrange("p (h n) -> p h n", h=2)
                             ).then_inc(S["side_read"], 1)
                if slot == GATE + 1:
                    gate_exponentials(img)
                if slot == GT:
                    store_gates(visit(b, "gT", 0), img)

            def hidden(i, e):
                z = ps[:, CH * (e % 2):CH * (e % 2) + CH, 0:UT]
                act.wait_ge(S["z_done"], i + 1)
                act.wait_ge(S["y_done"], i)
                act.activation(hh[e % 2], z, ACT.Gelu, scale=1.0 / WS).then_inc(S["hh_ready"], 1)
                act.activation(h32[e % 2], z, ACT.Gelu, scale=1.0 / WS).then_inc(S["h_ready"], 1)

            for r in range(G):
                n = visit(-1, "turn", r)
                act.wait_ge(S["side_done"], n + 1)
                act.copy(xhl[0:C, :, rowcols(0, r)],
                         ps[0:C, FIRST[n % 2], 0:UT].bitcast(F16).rearrange("p (h n) -> p h n", h=2)
                         ).then_inc(S["side_read"], 1)
            gate_exponentials(0)
            projected(B - 1)
            act.wait_ge(S["z_done"], 1)
            act.activation(hh[0], ps[:, 0:CH, 0:UT], ACT.Gelu, scale=1.0 / WS).then_inc(S["hh_ready"], 1)
            act.activation(h32[0], ps[:, 0:CH, 0:UT], ACT.Gelu, scale=1.0 / WS).then_inc(S["h_ready"], 1)
            store_gates(visit(-1, "gT", 0), 0)
            with act.Fori(0, B - 1) as b:
                act.wait_ge(S["x2_lo"], b * G + G)
                load_image(b + 1)
                for slot in range(SLOTS):
                    side(b, slot, b + 1)
                    hidden(b * SLOTS + (slot + 1), (slot + 1) % E)
            for slot in range(SLOTS - 1):
                hidden((B - 1) * SLOTS + slot + 1, (slot + 1) % E)

        @block.vector
        def _(dve):
            class Steps:

                def __init__(self, name):
                    self.sem, self.base, self.n = S[name], 0, 0

                def image(self, b, per):
                    assert self.n in (0, per), self.n
                    self.base, self.n = b * per, 0

                def mark(self, ins):
                    ins.then_inc(self.sem, 1)
                    self.n += 1

                def settle(self):
                    dve.wait_ge(self.sem, self.base + self.n)

                def link(self, ins):
                    self.mark(ins)
                    self.settle()

            s = Steps("zeros_step")
            s.mark(dve.memset(sf[:], 0.0))
            s.mark(dve.memset(sf16[:], 0.0))
            s.mark(dve.memset(zeros[:], 0.0))
            for n, (name, start) in enumerate((("y_done", 1), ("y_read", 1), ("h_ready", 1), ("sum_done", 2))):
                dve.memset(credit[:, n:n + 1], 0.0).then_inc(S[name], start)
            s.settle()

            def moments(s, eps, t0=0, t1=T):
                me, mo, qe, qo = (st[:, t0:t1, i] for i in (1, 4, 2, 5))
                m = [mom[:, i, t0:t1] for i in range(5)]
                s.mark(dve.tensor_tensor(m[1], me, mo, ALU.subtract))
                s.mark(dve.tensor_tensor(m[0], me, mo, ALU.add))
                s.link(dve.tensor_tensor(m[2], qe, qo, ALU.add))
                s.mark(dve.scalar_tensor_tensor(out=m[3], in0=m[1], scalar=0.25, in1=m[1], op0=ALU.mult,
                                                op1=ALU.mult))
                s.mark(dve.tensor_scalar(m[0], m[0], -0.5, None, ALU.mult))
                s.link(dve.tensor_scalar(m[2], m[2], 1.0 / C, eps, ALU.mult, ALU.add))
                dve.tensor_tensor(m[4], m[3], m[2], ALU.add).then_inc(S["moments_ready"], 1)

            def per_token(v, t0, t1):
                return v[:, t0:t1].unsqueeze(2).to_broadcast([PT, t1 - t0, C])

            def centre(img, r0, r1):
                t0, t1 = r0 * TU, r1 * TU
                return dve.tensor_tensor(img[:, t0:t1, :], img[:, t0:t1, :], per_token(mom[:, 0, :], t0, t1),
                                         ALU.add)

            def scale(img, r, ready):
                t0, t1 = r * TU, (r + 1) * TU
                dve.tensor_tensor(img[:, t0:t1, :], img[:, t0:t1, :], per_token(rstd, t0, t1), ALU.mult
                                  ).then_inc(ready, 1)

            def split_weights():
                s = Steps("weights_step")
                dve.wait_ge(S["consts_in"], 16 * N_CONST)
                for hi, lo, src in ((gate_hl[:, 0:E], gate_hl[:, E:2 * E], gate_st[:]),
                                    (w1_hi[:], w1_lo[:], w1_st),
                                    (w2_hi[:].rearrange("p a c -> p (a c)"),
                                     w2_lo[:].rearrange("p a c -> p (a c)"), w2_st)):
                    s.link(dve.tensor_scalar(hi, src, WS, None, ALU.mult))
                    s.mark(dve.scalar_tensor_tensor(out=lo, in0=src, scalar=WS, in1=hi, op0=ALU.mult,
                                                    op1=ALU.subtract))
                s.settle()
                dve.tensor_scalar(b2_sb[:], b2_sb[:], WS, None, ALU.mult).then_inc(S["weights_ready"], 1)
                dve.wait_ge(S["weights_ready"], 1)

            s = Steps("norm1_step")

            def statistics(b):
                for part, t0, t1 in (("a", 0, CUT * TU), ("b", CUT * TU, T)):
                    dve.wait_ge(S[f"x{part}_in{b % 3}"], 16 * (b // 3 + 1))
                    for t in range(t0, t1):
                        ins = dve.bn_stats(st[:, t, :], image(b)[:, t, 0:C])
                s.link(ins)

            def image_moments(b):
                if b > 0:
                    dve.wait_ge(S["xn_ready"], b * G)
                moments(s, 1e-6)

            def channels(b, r0, r1):
                for r in range(r0, r1):
                    z = ps[0:C, turn_bank("xn", b, r), 0:UT]
                    dve.wait_ge(S["hi_ready"], b * G + r + 1)
                    dve.tensor_tensor(xnC[:, 1, r * UT:(r + 1) * UT], z, xnC[:, 0, r * UT:(r + 1) * UT],
                                      ALU.subtract)
                    dve.tensor_reduce(sf[:, (r + 1) * GP + 1:(r + 1) * GP + 1 + G],
                                      z.rearrange("p (i j s) -> p j i s", i=SP, s=SP), AX.XY, ALU.add
                                      ).then_inc(S["lo_ready"], 1)

            def cells(b):
                grid = Steps("grid_step")
                grid.base = b
                dve.wait_ge(S["lo_ready"], b * G + G)
                inner_rows = slice(GP, GP * (G + 1))
                grid.link(dve.tensor_copy(sf16[:, 0, inner_rows], sf[:, inner_rows]))
                dve.tensor_tensor(sf16[:, 1, inner_rows], sf[:, inner_rows], sf16[:, 0, inner_rows], ALU.subtract
                                  ).then_inc(S["sf_ready"], 1)

            def centre_first_part(b):
                dve.wait_ge(S["moments_ready"], b + 1)
                centre(image(b)[:, :, 0:C], 0, CUT).then_inc(S["centred"], 1)

            statistics(0)
            image_moments(0)
            s.mark(centre(image(0)[:, :, 0:C], 0, G))
            statistics(1)
            dve.wait_ge(S["rstd_ready"], 1)
            for r in range(G):
                scale(image(0)[:, :, 0:C], r, S["xn_ready"])
            image_moments(1)
            channels(0, 0, G)
            cells(0)
            dve.tensor_copy(ident16[:], ident).then_inc(S["ident16_ready"], 1)
            centre_first_part(1)
            for b in range(B):
                if b > 0:
                    dve.wait_ge(S["aff_hi"], 2 * b)
                    dve.wait_ge(S["aff_lo"], b)
                for n, bank in enumerate(LOGITS):
                    dve.wait_ge(S["logits_done"], len(LOGITS) * b + n + 1)
                    t0, t1 = n * 2 * TU, min((n + 1) * 2 * TU, T)
                    tiles = aff[:, t0:t1, :]
                    z = ps[0:PT, bank, 0:(t1 - t0) * 2 * K9].rearrange("p (t h n) -> p t h n", h=2, n=K9)
                    s.link(dve.tensor_tensor(
                        tiles, z[:, :, 0, :], near[0:PT, :].unsqueeze(1).to_broadcast([PT, t1 - t0, K9]),
                        ALU.add))
                    s.mark(dve.tensor_tensor(tiles, z[:, :, 1, :], tiles, ALU.add))
                s.settle()
                s.link(dve.tensor_reduce(affs[:, 0, :], aff[:], AX.X, ALU.max))
                dve.tensor_tensor(aff[:], aff[:], affs[:, 0, :].unsqueeze(2).to_broadcast([PT, T, K9]),
                                  ALU.subtract).then_inc(S["shifted"], 1)
                if b + 1 < B:
                    channels(b + 1, 0, 1)
                dve.wait_ge(S["exp_ready"], b + 1)
                s.link(dve.tensor_reduce(affs[:, 1, :], aff[:], AX.X, ALU.add))
                s.link(dve.reciprocal(affs[:, 1, :], affs[:, 1, :]))
                dve.tensor_tensor(aff[:], aff[:], affs[:, 1, :].unsqueeze(2).to_broadcast([PT, T, K9]),
                                  ALU.mult).then_inc(S["aff_ready"], 1)
                if b + 1 < B:
                    channels(b + 1, 1, G)
                    cells(b + 1)
                if b + 2 < B:
                    statistics(b + 2)
                    image_moments(b + 2)
                    centre_first_part(b + 2)
                if b == B - 2:
                    split_weights()
                dve.wait_ge(S["sft_done"], b + 1)
                dve.tensor_copy(sft[:, bass.ds(b * N, N)].rearrange("p (i j) -> p i j", j=G),
                                ps[0:CB, SUPER, 0:GP * GP].rearrange("p (i j) -> p i j", j=GP)[:, 1:G + 1, 1:G + 1]
                                ).then_inc(S["sft_ready"], 1)

            s = Steps("attn_step")
            dve.wait_ge(S["init_done"], N_INIT)
            dve.wait_ge(S["super_turned"], 1)
            sT = ps[0:N, 0, 0:B * CB].rearrange("p (b c) -> p b c", b=B)
            s.link(dve.tensor_scalar(srec[:], sT[:, :, C], 1e-12, None, ALU.add))
            s.link(dve.reciprocal(srec[:], srec[:]))
            dve.tensor_tensor(sftT[:], sT[:, :, 0:C], srec[:].unsqueeze(2).to_broadcast([N, B, C]),
                              ALU.mult).then_inc(S["super_ready"], 1)
            dve.memset(q[:, :, B * N:QW], 0.0)
            dve.wait_ge(S["superT_done"], 1)
            dve.tensor_copy(sfn[:], ps[0:C, 1, 0:B * N].rearrange("p (b n) -> p b n", b=B)
                            ).then_inc(S["superT_ready"], 1)
            dve.wait_ge(S["qk_done"], 1)
            dve.tensor_copy(q[:, :, 0:B * N], ps[:, 5, 0:GROUPS * B * N].rearrange("p (g n) -> p g n", g=GROUPS)
                            ).then_inc(S["q_ready"], 1)
            dve.wait_ge(S["v_done"], 1)
            dve.tensor_copy(vT[:, :, :, 0:HD].rearrange("n b h d -> n (b h) d"),
                            ps[0:N, VALUES, 0:B * C].rearrange("n (g d) -> n g d", d=HD)).then_inc(S["v_ready"], 1)

            def shift_scores(p):
                dve.wait_ge(S["scores_done"], p + 1)
                scores = ps[:, 0:4, 0:GROUPS * N].rearrange("p r (g n) -> p r g n", n=N)
                top = peak[:, p, :].rearrange("p (r g) -> p r g", g=GROUPS)
                s.link(dve.tensor_reduce(top, scores, AX.X, ALU.max))
                dve.tensor_tensor(prob[:, p, :, :].rearrange("p (g r) n -> p r g n", g=GROUPS), scores,
                                  top.unsqueeze(3).to_broadcast([128, 4, GROUPS, N]), ALU.subtract
                                  ).then_inc(S["scores_shifted"], 1)

            def finish_heads(p):
                dve.wait_ge(S["heads_done"], p + 1)
                g0, g1 = p * 2 * HEADS, (p + 1) * 2 * HEADS
                heads = ps[0:N, 2, g0 * (HD + 1):g1 * (HD + 1)].rearrange("n (g d) -> n g d", d=HD + 1)
                s.link(dve.reciprocal(arec[:, g0:g1], heads[:, :, HD]))
                dve.tensor_tensor(ao[:, 2 * p:2 * p + 2, :].rearrange("p b (h d) -> p (b h) d", h=HEADS),
                                  heads[:, :, 0:HD], arec[:, g0:g1].unsqueeze(2).to_broadcast([N, g1 - g0, HD]),
                                  ALU.mult).then_inc(S["heads_ready"], 1)
                dve.wait_ge(S["headsT_done"], p + 1)
                for b in (2 * p, 2 * p + 1):
                    dve.tensor_copy(
                        aoT[0:C, b, 0:GP * GP].rearrange("p (i j) -> p i j", j=GP)[:, 1:G + 1, 1:G + 1],
                        ps[0:C, 3, b * N:(b + 1) * N].rearrange("p (i j) -> p i j", j=G)
                        ).then_inc(S["headsT_ready"], 1)

            shift_scores(0)
            dve.wait_ge(S["probT_done"], 1)
            dve.tensor_copy(probT_pair(0), probT_psum()).then_inc(S["probT_ready0"], 1)
            finish_heads(0)

            def projected(b):
                dve.wait_ge(S["so_hi"], 2 * b + 1)
                for bank, rows in banks_of(b):
                    units = slice(b * G + rows[0], b * G + rows[-1] + 1)
                    ins = dve.tensor_tensor(so[2 * ZONE:3 * ZONE, units, :],
                                            ps[0:ZONE, bank, 0:len(rows) * C].rearrange("p (n c) -> p n c", c=C),
                                            so[0:ZONE, units, :], ALU.subtract)
                ins.then_inc(S["so_lo"], 1)

            s = Steps("norm3_step")
            PER = 24

            def add_pixels(n, r, bank):
                dve.wait_ge(S["side_done"], n + 1)
                rows = xm[:, r * TU:(r + 1) * TU, :]
                dve.tensor_tensor(rows, rows, ps[0:PT, bank, 0:TU * C].rearrange("p (t c) -> p t c", c=C),
                                  ALU.add).then_inc(S["side_read"], 1)

            def pixel_statistics(n, r):
                dve.wait_ge(S["side_read"], n + 1)
                for t in range(r * TU, (r + 1) * TU):
                    ins = dve.bn_stats(st[:, t, :], xm[:, t, :])
                return ins

            def side_first(b, slot, img):
                r = slot - PIX
                if 0 <= r < G:
                    if r == 0:
                        s.image(b, PER)
                    if r in (0, CUT):
                        dve.wait_ge(S[f"xm_in{r // CUT}"], img * 16 + 16)
                    add_pixels(visit(b, "pix", r), r, SIDE)

            def low_tokens(img, r):
                dve.wait_ge(S["x2_hi"], img * G + (r + 1))
                dve.wait_ge(S["x2_ready"], img * G + (r + 1))
                rows = slice(r * TU, (r + 1) * TU)
                dve.tensor_tensor(x16[:, rows, 1, :], xm[:, rows, :], x16[:, rows, 0, :], ALU.subtract
                                  ).then_inc(S["x2_lo"], 1)

            def side_last(b, slot, img):
                r = slot - PIX
                if 0 <= r < G:
                    ins = pixel_statistics(visit(b, "pix", r), r)
                    if r == G - 1:
                        s.link(ins)
                if slot == MEAN:
                    moments(s, 1e-5)
                    dve.wait_ge(S["moments_ready"], img + (B + 2))
                for step, (r0, r1) in enumerate(((0, 2), (2, 4), (4, G))):
                    if slot == MEAN + step:
                        s.mark(centre(xm, r0, r1))
                r = slot - SCALE
                if 0 <= r < G:
                    if r == 0:
                        s.settle()
                        dve.wait_ge(S["rstd_ready"], img + (B + 2))
                    scale(xm, r, S["x2_ready"])
                r = slot - SCALE - 1
                if 0 <= r < G:
                    low_tokens(img, r)
                if slot == GATE + 1:
                    gate_probabilities(img)
                if slot == GATE + 2:
                    gate_pairs()
                if slot == GATE + 3:
                    gate_ranks()
                if slot == GATE + 4:
                    gate_chosen()
                if slot == GATE + 5:
                    gate_weights()

            def over_experts(v):
                return v.unsqueeze(2).to_broadcast([PT, T, E])

            def gate_logits(n, img, bank):
                dve.wait_ge(S["side_done"], n + 1)
                dve.tensor_reduce(gl[:], ps[0:PT, bank, 0:2 * T * E].rearrange("p (t h e) -> p t e h", h=2, e=E),
                                  AX.X, ALU.add).then_inc(S["side_read"], 1)
                dve.wait_ge(S["side_read"], n + 1)
                s.link(dve.tensor_reduce(gs[:, 0, :], gl[:], AX.X, ALU.max))
                dve.tensor_tensor(gl[:], gl[:], over_experts(gs[:, 0, :]), ALU.subtract
                                  ).then_inc(S["gate_shifted"], 1)

            pair = gc[:].rearrange("p t (e j) -> p t e j", e=E)

            def gate_probabilities(img):
                dve.wait_ge(S["gate_exp"], img + 1)
                s.link(dve.tensor_reduce(gs[:, 1, :], gl[:], AX.X, ALU.add))
                s.link(dve.reciprocal(gs[:, 1, :], gs[:, 1, :]))
                s.link(dve.tensor_tensor(gl[:], gl[:], over_experts(gs[:, 1, :]), ALU.mult))

            def gate_pairs():
                s.link(dve.tensor_tensor(pair, gl[:].unsqueeze(2).to_broadcast([PT, T, E, E]),
                                         gl[:].unsqueeze(3).to_broadcast([PT, T, E, E]), ALU.is_ge))
                s.link(dve.tensor_tensor(gc[:], gc[:], below[0:PT, :].unsqueeze(1).to_broadcast([PT, T, E * E]),
                                         ALU.mult))

            def gate_ranks():
                s.mark(dve.tensor_reduce(ga[:, 0, :, :], pair, AX.X, ALU.add))
                s.link(dve.tensor_reduce(ga[:, 1, :, :], gc[:].rearrange("p t (e j) -> p t j e", e=E), AX.X,
                                         ALU.add))
                s.link(dve.tensor_tensor(ga[:, 0, :, :], ga[:, 0, :, :], ga[:, 1, :, :], ALU.subtract))

            def gate_chosen():
                s.link(dve.tensor_tensor(ga[:, 0, :, :], ga[:, 0, :, :],
                                         rankmax[0:PT, :].unsqueeze(1).to_broadcast([PT, T, E]), ALU.is_lt))
                s.link(dve.tensor_tensor(gl[:], gl[:], ga[:, 0, :, :], ALU.mult))

            def gate_weights():
                s.link(dve.tensor_reduce(gs[:, 2, :], gl[:], AX.X, ALU.add))
                s.link(dve.tensor_scalar(gs[:, 2, :], gs[:, 2, :], WS, WS * 1e-9, ALU.mult, ALU.add))
                s.link(dve.reciprocal(gs[:, 2, :], gs[:, 2, :]))
                dve.tensor_tensor(gl[:], gl[:], over_experts(gs[:, 2, :]), ALU.mult
                                  ).then_inc(S["gate_ready"], 1)

            def low_part(i, e):
                dve.wait_ge(S["h_ready"], i + 2)
                dve.tensor_tensor(hl[e % 2], h32[e % 2], hh[e % 2], ALU.subtract).then_inc(S["hl_ready"], 1)

            def residual(b, r):
                dve.wait_ge(S[f"unit_in{buf(r)}"], uses(b, r) * 32)
                dve.wait_ge(S["side_done"], visit(b, "res", r) + 1)
                dve.tensor_tensor(res[buf(r)][:], res[buf(r)][:], ps[0:C, SIDE, 0:UT], ALU.add
                                  ).then_inc(S["side_read"], 1)

            def weigh(i, r, e):
                dve.wait_ge(S["y_done"], i + 2)
                dve.wait_ge(S["sum_done"], i + 1)
                dve.scalar_tensor_tensor(out=acc[e % 2][:], in0=ps[0:C, Y, 0:UT], scalar=b2_sb[:, e:e + 1],
                                         in1=gb[buf(r)][:, e, :], op0=ALU.add, op1=ALU.mult
                                         ).then_inc(S["y_read"], 1)

            def experts(b, last):
                for slot in range(SLOTS):
                    r, e = divmod(slot, E)
                    i = b * SLOTS + slot
                    if not last:
                        side_first(b, slot, b + 1)
                    low_part(i, e)
                    if not last and slot == GATE:
                        gate_logits(visit(b, "gate", 0), b + 1, SIDE)
                    if e == 0:
                        residual(b, r)
                    if not last:
                        side_last(b, slot, b + 1)
                    weigh(i, r, e)

            steady, s = s, Steps("norm2_step")
            projected(0)
            for r in range(G):
                if r in (0, CUT):
                    dve.wait_ge(S[f"xm_in{r // CUT}"], 16)
                n = visit(-1, "pix", r)
                add_pixels(n, r, FIRST[n % 2])
                ins = pixel_statistics(n, r)
                if r == 1:
                    shift_scores(1)
                if r == CUT - 1:
                    s.link(ins)
                    moments(s, 1e-5, 0, CUT * TU)
            s.link(ins)
            moments(s, 1e-5, CUT * TU, T)
            for part, (r0, r1) in enumerate(((0, CUT), (CUT, G))):
                dve.wait_ge(S["moments_ready"], B + 1 + part)
                s.mark(centre(xm, r0, r1))
                if part == 0:
                    finish_heads(1)
            s.settle()
            for r in range(G):
                dve.wait_ge(S["rstd_ready"], B + 1 + r // CUT)
                scale(xm, r, S["x2_ready"])
                if r > 0:
                    low_tokens(0, r - 1)
                if r in (3, 5):
                    projected((r - 1) // 2)
            low_tokens(0, G - 1)
            gate_logits(visit(-1, "gate", 0), 0, FIRST_GATE)
            gate_probabilities(0)
            gate_pairs()
            gate_ranks()
            gate_chosen()
            gate_weights()
            projected(B - 1)
            s = steady
            with dve.Fori(0, B - 1) as b:
                experts(b, False)
            experts(B - 1, True)

        @block.tensor
        def _(pe):
            pe.wait_ge(S["consts_in"], 16 * N_CONST)

            def free_bank(kind, b, r):
                before = turn_before(kind, b, r)
                if before is not None:
                    kind0, b0, r0 = before
                    pe.wait_ge(S["lo_ready" if kind0 == "xn" else "affT_ready"], b0 * G + r0 + 1)

            def channels(b, r):
                pe.wait_ge(S["xn_ready"], b * G + r + 1)
                free_bank("xn", b, r)
                for j in range(TU):
                    ins = pe.transpose(ps[0:C, turn_bank("xn", b, r), j * PT:(j + 1) * PT],
                                       image(b)[:, r * TU + j, 0:C], ident[0:PT, 0:PT])
                ins.then_inc(S["xnC_done"], 1)

            def logits(b):
                pe.wait_ge(S["sf_ready"], b + 1)
                for r in range(G):
                    for j in range(TU):
                        t = r % 2 * TU + j
                        c0 = r * UT + j * PT
                        for half in range(2):
                            ins = pe.matmul(ps[0:PT, LOGITS[r // 2], t * 2 * K9:(t + 1) * 2 * K9],
                                            xnC[:, half, c0:c0 + PT], sf16[:, :, r * GP:r * GP + K9],
                                            start=(half == 0), stop=(half == 1))
                    if r % 2 == 1 or r == G - 1:
                        ins.then_inc(S["logits_done"], 1)

            def turn_affinities(b, r):
                pe.wait_ge(S["aff_hi"], b * 2 + 2)
                pe.wait_ge(S["aff_lo"], b + 1)
                pe.wait_ge(S["ident16_ready"], 1)
                for j in range(TU):
                    columns = slice(j * PT // 2, (j + 1) * PT // 2)
                    ins = pe.transpose(ps[0:3 * ZONE, turn_bank("aff", b, r), columns].bitcast(F16),
                                       aff16[:, r * TU + j, :], ident16[0:PT, 0:PT])
                ins.then_inc(S["affT_done"], 1)

            for r in range(G):
                channels(0, r)
            logits(0)
            for b in range(B):
                if b + 1 < B:
                    for r in range(TURNS + 1):
                        channels(b + 1, r)
                pe.wait_ge(S["aff_ready"], b + 1)
                if b > 0:
                    pe.wait_ge(S["sft_ready"], b)
                pe.matmul(ps[0:CB, SUPER, 0:GP * GP], zeros[:], ident[0:PT, 0:GP * GP], start=True, stop=False,
                          skip_group_check=True)
                for r in range(G):
                    for t in range(r * TU, (r + 1) * TU):
                        ins = pe.matmul(ps[0:CB, SUPER, r * GP:r * GP + K9], image(b)[:, t, :], aff[:, t, :],
                                        start=False, stop=(t == T - 1), skip_group_check=True)
                    if b + 1 < B and TURNS + 1 + r < G:
                        channels(b + 1, TURNS + 1 + r)
                ins.then_inc(S["sft_done"], 1)
                if b + 1 < B:
                    logits(b + 1)
                if b < B - 1:
                    for r in range(G):
                        free_bank("aff", b, r)
                        turn_affinities(b, r)
            pe.wait_ge(S["sft_ready"], B)
            pe.wait_ge(S["affT_ready"], (B - 1) * G)

            for b in range(B):
                ins = pe.transpose(ps[0:N, 0, b * CB:(b + 1) * CB], sft[:, b * N:(b + 1) * N], ident[0:CB, 0:CB])
            ins.then_inc(S["super_turned"], 1)
            pe.wait_ge(S["super_ready"], 1)
            for b in range(B):
                ins = pe.transpose(ps[0:C, 1, b * N:(b + 1) * N], sftT[:, b, :], ident[0:N, 0:N])
            ins.then_inc(S["superT_done"], 1)
            pe.wait_ge(S["superT_ready"], 1)
            for which in range(2):
                for g in range(GROUPS):
                    w0 = (which * GROUPS + g) * 128
                    ins = pe.matmul(ps[:, 5 + which, g * B * N:(g + 1) * B * N], wqkv_sb[:, w0:w0 + 128],
                                    sfn[:].rearrange("p b n -> p (b n)"), start=True, stop=True)
            ins.then_inc(S["qk_done"], 1)
            for b in range(B):
                ins = pe.matmul(ps[0:N, VALUES, b * C:(b + 1) * C], sfn[:, b, :], wqkv_sb[:, 2 * HEADS * ZONE:],
                                start=True, stop=True)
            ins.then_inc(S["v_done"], 1)
            pe.wait_ge(S["q_ready"], 1)
            pe.wait_ge(S["k_ready"], 1)

            def scores(p):
                for b in (2 * p, 2 * p + 1):
                    for h in range(HEADS):
                        g, rows = h // 4, slice(h % 4 * ZONE, h % 4 * ZONE + HD)
                        out0, c0 = b % 2 * HALF, g * N
                        ins = pe.matmul(ps[out0:out0 + HALF, h % 4, c0:c0 + N],
                                        q[rows, g, b * N:b * N + HALF], k[rows, g, b * N:(b + 1) * N],
                                        start=True, stop=True)
                ins.then_inc(S["scores_done"], 1)

            def turn_probabilities(p):
                pe.wait_ge(S["prob_ready"], p + 1)
                for h in range(HEADS):
                    c0 = h % 4 * 128
                    ins = pe.transpose(ps[0:N, h // 4, c0:c0 + 128], prob[:, p, h, :], ident)
                ins.then_inc(S["probT_done"], 1)

            def heads(p):
                pe.wait_ge(S[f"probT_ready{p}"], 1)
                for b in (2 * p, 2 * p + 1):
                    for h in range(HEADS):
                        c0 = (b * HEADS + h) * (HD + 1)
                        ins = pe.matmul(ps[0:N, 2, c0:c0 + HD + 1], probT[:, b, h, :], vT[:, b, h, :],
                                        start=True, stop=True)
                ins.then_inc(S["heads_done"], 1)

            def turn_heads(p):
                pe.wait_ge(S["heads_ready"], p + 1)
                for b in (2 * p, 2 * p + 1):
                    ins = pe.transpose(ps[0:C, 3, b * N:(b + 1) * N], ao[:, b, :], ident[0:N, 0:N])
                ins.then_inc(S["headsT_done"], 1)

            def turn_last_affinities(r0, r1):
                for r in range(r0, r1):
                    if r >= 2:
                        pe.wait_ge(S["affT_ready"], (B - 1) * G + r - 1)
                    turn_affinities(B - 1, r)

            scores(0)
            turn_last_affinities(0, 2)
            turn_probabilities(0)
            turn_last_affinities(2, 4)
            heads(0)
            turn_last_affinities(4, 6)
            turn_heads(0)
            turn_last_affinities(6, G)

            def project(b):
                pe.wait_ge(S["headsT_ready"], b + 1)
                if b in (1, 3):
                    pe.wait_ge(S["so_lo"], (b + 1) // 2)
                for bank, rows in banks_of(b):
                    for n, r in enumerate(rows):
                        ins = pe.matmul(ps[0:ZONE, bank, n * C:(n + 1) * C], aoT[:, b, r * GP:r * GP + ZONE],
                                        wproj_sb[:], start=True, stop=True)
                ins.then_inc(S["proj_done"], 1)

            pe.wait_ge(S["affT_ready"], B * G - 1)
            project(0)

            def pixels(img, r, bank):
                turned = affT[:, rowcols(img, r)]
                super_tokens = so[:, bass.ds(img * G + r, 1), :].rearrange("p o c -> p (o c)")
                for j in range(TU):
                    ins = pe.matmul(ps[0:PT, bank, j * C:(j + 1) * C], turned[:, j * PT:(j + 1) * PT],
                                    super_tokens, start=True, stop=True)
                return ins

            def turn(img, r, bank):
                pe.wait_ge(S["x2_hi"], img * G + (r + 1))
                pe.wait_ge(S["x2_lo"], img * G + (r + 1))
                for half in range(2):
                    for j in range(TU):
                        c0 = (half * UT + j * PT) // 2
                        ins = pe.transpose(ps[0:C, bank, c0:c0 + PT // 2].bitcast(F16),
                                           x16[:, r * TU + j, half, :], ident16[0:PT, 0:PT])
                return ins

            def gate(img, r, bank):
                tokens = xhl[:, :, rowcols(img, r)]
                for j in range(TU):
                    t = r * TU + j
                    for half in range(2):
                        ins = pe.matmul(ps[0:PT, bank, t * 2 * E:(t + 1) * 2 * E],
                                        tokens[:, half, j * PT:(j + 1) * PT], gate_hl[:],
                                        start=(half == 0), stop=(half == 1))
                return ins

            def turn_gates(img):
                pe.wait_ge(S["gate_ready"], img + 1)
                return pe.transpose(ps[0:T * E, SIDE, 0:PT], gl[:].rearrange("p t e -> p (t e)"),
                                    ident[0:PT, 0:PT])

            def side(b, slot, img):
                if slot not in early:
                    return
                kind, r = early[slot]
                n = visit(b, kind, r)
                pe.wait_ge(S["side_read"], n)
                if kind == "pix":
                    ins = pixels(img, r, SIDE)
                elif kind == "turn":
                    ins = turn(img, r, SIDE)
                elif kind == "gate":
                    for unit in range(G):
                        ins = gate(img, unit, SIDE)
                else:
                    ins = turn_gates(img)
                ins.then_inc(S["side_done"], 1)

            def residual(b, r):
                pe.wait_ge(S["side_read"], visit(b, "res", r))
                pe.matmul(ps[0:C, SIDE, 0:UT], so[:, bass.ds(b * G + r, 1), :].rearrange("p o c -> p (o c)"),
                          affT[:, rowcols(b, r)], start=True, stop=True).then_inc(S["side_done"], 1)

            def first_layer(b, r, e):
                for c in range(CH):
                    w0 = e * HID + c * 128
                    for n, (ww, half) in enumerate(((w1_hi, 0), (w1_hi, 1), (w1_lo, 0))):
                        ins = pe.matmul(ps[:, CH * (e % 2) + c, 0:UT], ww[:, w0:w0 + 128],
                                        xhl[:, half, rowcols(b, r)], start=(n == 0), stop=(n == 2))
                ins.then_inc(S["z_done"], 1)

            def second_layer(i, e):
                y = ps[0:C, Y, 0:UT]
                pe.wait_ge(S["y_read"], i + 1)
                pe.wait_ge(S["hh_ready"], i + 1)
                for c in range(CH):
                    pe.matmul(y, w2_hi[:, e * CH + c, :], hh[e % 2][:, c, :], start=(c == 0), stop=False)
                    pe.matmul(y, w2_lo[:, e * CH + c, :], hh[e % 2][:, c, :], start=False, stop=False)
                pe.wait_ge(S["hl_ready"], i + 1)
                for c in range(CH):
                    ins = pe.matmul(y, w2_hi[:, e * CH + c, :], hl[e % 2][:, c, :], start=False,
                                    stop=(c == CH - 1))
                ins.then_inc(S["y_done"], 1)

            def experts(b, last):
                for slot in range(SLOTS):
                    r, e = divmod(slot, E)
                    i = b * SLOTS + slot
                    if not last:
                        side(b, slot, b + 1)
                    if not last or slot < SLOTS - 1:
                        pe.wait_ge(S["h_ready"], i + 1)
                        r1, e1 = divmod(slot + 1, E)
                        first_layer(b if r1 < G else b + 1, r1 % G, e1)
                    if e == 0:
                        residual(b, r)
                    second_layer(i, e)

            pe.wait_ge(S["headsT_ready"], 2)
            scores(1)
            pe.wait_ge(S["v_ready"], 1)
            pe.wait_ge(S["affT_ready"], B * G)
            pe.wait_ge(S["so_lo"], 1)
            pe.wait_ge(S["so_hi"], 2)
            for r in range(G):
                n = visit(-1, "pix", r)
                if n >= 2:
                    pe.wait_ge(S["side_read"], n - 1)
                pixels(0, r, FIRST[n % 2]).then_inc(S["side_done"], 1)
                if r == 4:
                    turn_probabilities(1)
            heads(1)
            project(1)
            turn_heads(1)
            project(2)
            pe.wait_ge(S["headsT_ready"], B)
            pe.wait_ge(S["pool_init"], N_POOL)
            pe.wait_ge(S["weights_ready"], 1)
            for r in range(G):
                n = visit(-1, "turn", r)
                pe.wait_ge(S["side_read"], n - 1)
                turn(0, r, FIRST[n % 2]).then_inc(S["side_done"], 1)
                if r > 0:
                    pe.wait_ge(S["side_read"], n)
                    gate(0, r - 1, FIRST_GATE)
            pe.wait_ge(S["side_read"], n + 1)
            gate(0, G - 1, FIRST_GATE).then_inc(S["side_done"], 1)
            project(B - 1)
            pe.wait_ge(S["so_lo"], B - 1)
            first_layer(0, 0, 0)
            turn_gates(0).then_inc(S["side_done"], 1)
            pe.wait_ge(S["so_lo"], B)
            pe.wait_ge(S["so_hi"], 2 * B)
            with pe.Fori(0, B - 1) as b:
                experts(b, False)
            experts(B - 1, True)


def kernel(x, L0_conv_xl, L0_conv_qkv_w, L0_conv_proj_w, L0_conv_proj_b, L0_ffn_gate_w, L0_ffn_gate_b, L0_ffn_w1,
           L0_ffn_b1, L0_ffn_w2, L0_ffn_b2):
    import concourse.bacc as bacc
    from concourse.bass_utils import run_bass_kernel_spmd

    def lay(a):
        return np.ascontiguousarray(np.asarray(a))

    table, inner = constants()
    wqkv = np.asarray(L0_conv_qkv_w).reshape(HEADS, 3, HD, C).transpose(3, 1, 0, 2)
    wqk = np.zeros((C, 2, HEADS, ZONE), np.float32)
    wqk[:, :, :, 0:HD] = wqkv[:, 0:2]
    wqkv = np.concatenate([wqk.reshape(C, -1), wqkv[:, 2].reshape(C, C)], axis=1)
    arrays = {
        "x": lay(np.asarray(x).transpose(1, 0, 2, 3).reshape(C, TOK)),
        "xtok": lay(np.concatenate([np.asarray(x).reshape(B, C, T, PT).transpose(3, 0, 2, 1),
                                    np.ones((PT, B, T, 1), np.float32)], axis=3)),
        "table": table,
        "inner": inner,
        "wqkv": lay(wqkv),
        "wproj": lay(np.asarray(L0_conv_proj_w).T),
        "bproj": lay(L0_conv_proj_b).reshape(1, C),
        "gate_w": lay(L0_ffn_gate_w),
        "gate_b": lay(L0_ffn_gate_b).reshape(1, E),
        "w1": lay(np.asarray(L0_ffn_w1).transpose(1, 0, 2).reshape(C, E * HID)),
        "b1": lay(L0_ffn_b1).reshape(1, E * HID),
        "w2": lay(np.asarray(L0_ffn_w2).reshape(E, CH, 128, C).transpose(2, 0, 1, 3).reshape(128, E * CH * C)),
        "b2": lay(np.asarray(L0_ffn_b2).T),
    }
    nc = bacc.Bacc("TRN2", target_bir_lowering=False, num_devices=1)
    args = [nc.dram_tensor(n, a.shape, mybir.dt.from_np(a.dtype), kind="ExternalInput").ap()
            for n, a in arrays.items()]
    gates = nc.dram_tensor("gates", [E, TOK], F32, kind="Internal").ap()
    out = nc.dram_tensor("out", [C, TOK], F32, kind="ExternalOutput").ap()
    build(nc, *args, gates, out)
    r = run_bass_kernel_spmd(nc, [arrays], core_ids=[0])
    return r.results[0]["out"].reshape(C, B, H, W).transpose(1, 0, 2, 3)
```
